# Optimizing a Trainium2 kernel written in Bass

```python
import numpy as np
import jax
import jax.numpy as jnp

def _softmax(x, axis=-1):
    return jax.nn.softmax(x, axis=axis)

def _gelu(x):
    return jax.nn.gelu(x, approximate=True)

def _silu(x):
    return jax.nn.silu(x)

def _sigmoid(x):
    return jax.nn.sigmoid(x)

def _layernorm(x, axis=-1, eps=1e-05):
    m = jnp.mean(x, axis=axis, keepdims=True)
    v = jnp.var(x, axis=axis, keepdims=True)
    return (x - m) / jnp.sqrt(v + eps)

def _scatter_add(tgt, idx, src, axis=0):
    return tgt.at[idx].add(src)

def _segment_sum(src, seg, n):
    return jax.ops.segment_sum(src, seg, n)
kernel_name = 'mk_seq_postln_d1_jaxref_r4_48e3b0'

def setup_inputs(seed: int=0):
    np.random.seed(seed)
    _w = jnp.asarray

    def _L0_attn_setup():
        import jax, jax.numpy as jnp
        import numpy as np
        DIM = 512
        N_HEADS = 16
        HEAD_DIM = DIM // N_HEADS
        GROUP_SIZE = 128
        THRESHOLD = 0.5
        EPS = 1e-08
        B, T = (2, 512)

        def _ternary_dequant(w):
            O, I = w.shape
            g = I // GROUP_SIZE
            wg = w.reshape(O, g, GROUP_SIZE)
            scale = jnp.clip(jnp.mean(jnp.abs(wg), axis=-1, keepdims=True), EPS)
            wn = wg / scale
            q = jnp.where(wn > THRESHOLD, 1.0, jnp.where(wn < -THRESHOLD, -1.0, 0.0))
            return (q * scale).reshape(O, I)

        def _bitlinear(x, w):
            w_ste = w + jax.lax.stop_gradient(_ternary_dequant(w) - w)
            return x @ w_ste.T

        def _rope_tables(t, head_dim, base=10000.0):
            half = head_dim // 2
            inv_freq = 1.0 / base ** (jnp.arange(half, dtype=jnp.float32) / half)
            freqs = jnp.outer(jnp.arange(t, dtype=jnp.float32), inv_freq)
            return (jnp.cos(freqs), jnp.sin(freqs))

        def _apply_rope(x, cos, sin):
            d = x.shape[-1]
            x1, x2 = (x[..., :d // 2], x[..., d // 2:])
            cos = cos[None, None, :, :]
            sin = sin[None, None, :, :]
            return jnp.concatenate([x1 * cos - x2 * sin, x1 * sin + x2 * cos], axis=-1)
        key = jax.random.key(seed)
        ks = jax.random.split(key, 5)
        std = 1.0 / np.sqrt(DIM)
        return {'x': jax.random.normal(ks[0], (B, T, DIM), dtype=jnp.float32), 'w_q': jax.random.normal(ks[1], (DIM, DIM), dtype=jnp.float32) * std, 'w_k': jax.random.normal(ks[2], (DIM, DIM), dtype=jnp.float32) * std, 'w_v': jax.random.normal(ks[3], (DIM, DIM), dtype=jnp.float32) * std, 'w_o': jax.random.normal(ks[4], (DIM, DIM), dtype=jnp.float32) * std}
    _L0_attn_in = _L0_attn_setup()

    def _L0_ffn_setup():
        import jax, jax.numpy as jnp
        import numpy as np
        HIDDEN = 512
        INTER = 2048
        B, S = (4, 256)

        def _qmatmul(x, w_int8, scale):
            y = jnp.einsum('bsh,ho->bso', x, w_int8.astype(x.dtype))
            return y * scale
        key = jax.random.key(seed)
        ks = jax.random.split(key, 7)
        x = jax.random.normal(ks[0], (B, S, HIDDEN), dtype=jnp.float32)
        w_gate = jax.random.randint(ks[1], (HIDDEN, INTER), -128, 128, dtype=jnp.int32).astype(jnp.int8)
        w_up = jax.random.randint(ks[2], (HIDDEN, INTER), -128, 128, dtype=jnp.int32).astype(jnp.int8)
        w_down = jax.random.randint(ks[3], (INTER, HIDDEN), -128, 128, dtype=jnp.int32).astype(jnp.int8)
        s_gate = jax.random.uniform(ks[4], (INTER,), dtype=jnp.float32) * 0.02 + 0.001
        s_up = jax.random.uniform(ks[5], (INTER,), dtype=jnp.float32) * 0.02 + 0.001
        s_down = jax.random.uniform(ks[6], (HIDDEN,), dtype=jnp.float32) * 0.02 + 0.001
        return {'x': x, 'w_gate': w_gate, 'w_up': w_up, 'w_down': w_down, 's_gate': s_gate, 's_up': s_up, 's_down': s_down}
    _L0_ffn_in = _L0_ffn_setup()
    _d = {'L0_attn_x': _L0_attn_in['x'], 'L0_attn_w_q': _L0_attn_in['w_q'], 'L0_attn_w_k': _L0_attn_in['w_k'], 'L0_attn_w_v': _L0_attn_in['w_v'], 'L0_attn_w_o': _L0_attn_in['w_o'], 'L0_ffn_w_gate': _L0_ffn_in['w_gate'], 'L0_ffn_w_up': _L0_ffn_in['w_up'], 'L0_ffn_w_down': _L0_ffn_in['w_down'], 'L0_ffn_s_gate': _L0_ffn_in['s_gate'], 'L0_ffn_s_up': _L0_ffn_in['s_up'], 'L0_ffn_s_down': _L0_ffn_in['s_down']}
    _x0 = _d['L0_attn_x']
    _d['L0_attn_x'] = jax.random.normal(jax.random.fold_in(jax.random.key(seed), 1), (1, 2048, 512), dtype=_x0.dtype)
    del _x0
    return _d

def reference(L0_attn_x, L0_attn_w_q, L0_attn_w_k, L0_attn_w_v, L0_attn_w_o, L0_ffn_w_gate, L0_ffn_w_up, L0_ffn_w_down, L0_ffn_s_gate, L0_ffn_s_up, L0_ffn_s_down):

    def _L0_attn_ref(x, w_q, w_k, w_v, w_o):
        import jax, jax.numpy as jnp
        import numpy as np
        DIM = 512
        N_HEADS = 16
        HEAD_DIM = DIM // N_HEADS
        GROUP_SIZE = 128
        THRESHOLD = 0.5
        EPS = 1e-08
        B, T = (2, 512)

        def _ternary_dequant(w):
            O, I = w.shape
            g = I // GROUP_SIZE
            wg = w.reshape(O, g, GROUP_SIZE)
            scale = jnp.clip(jnp.mean(jnp.abs(wg), axis=-1, keepdims=True), EPS)
            wn = wg / scale
            q = jnp.where(wn > THRESHOLD, 1.0, jnp.where(wn < -THRESHOLD, -1.0, 0.0))
            return (q * scale).reshape(O, I)

        def _bitlinear(x, w):
            w_ste = w + jax.lax.stop_gradient(_ternary_dequant(w) - w)
            return x @ w_ste.T

        def _rope_tables(t, head_dim, base=10000.0):
            half = head_dim // 2
            inv_freq = 1.0 / base ** (jnp.arange(half, dtype=jnp.float32) / half)
            freqs = jnp.outer(jnp.arange(t, dtype=jnp.float32), inv_freq)
            return (jnp.cos(freqs), jnp.sin(freqs))

        def _apply_rope(x, cos, sin):
            d = x.shape[-1]
            x1, x2 = (x[..., :d // 2], x[..., d // 2:])
            cos = cos[None, None, :, :]
            sin = sin[None, None, :, :]
            return jnp.concatenate([x1 * cos - x2 * sin, x1 * sin + x2 * cos], axis=-1)
        b, t, c = x.shape
        scale = HEAD_DIM ** (-0.5)

        def split_heads(y):
            return y.reshape(b, t, N_HEADS, HEAD_DIM).transpose(0, 2, 1, 3)
        q = split_heads(_bitlinear(x, w_q))
        k = split_heads(_bitlinear(x, w_k))
        v = split_heads(_bitlinear(x, w_v))
        cos, sin = _rope_tables(t, HEAD_DIM)
        q = _apply_rope(q, cos, sin)
        k = _apply_rope(k, cos, sin)
        scores = jnp.einsum('bhqd,bhkd->bhqk', q, k) * scale
        causal = jnp.triu(jnp.ones((t, t), dtype=bool), k=1)
        scores = jnp.where(causal[None, None], -jnp.inf, scores)
        probs = jax.nn.softmax(scores, axis=-1)
        y = jnp.einsum('bhqk,bhkd->bhqd', probs, v)
        y = y.transpose(0, 2, 1, 3).reshape(b, t, c)
        return _bitlinear(y, w_o)

    def _L0_ffn_ref(x, w_gate, w_up, w_down, s_gate, s_up, s_down):
        import jax, jax.numpy as jnp
        import numpy as np
        HIDDEN = 512
        INTER = 2048
        B, S = (4, 256)

        def _qmatmul(x, w_int8, scale):
            y = jnp.einsum('bsh,ho->bso', x, w_int8.astype(x.dtype))
            return y * scale
        gate = jax.nn.silu(_qmatmul(x, w_gate, s_gate))
        up = _qmatmul(x, w_up, s_up)
        fuse = gate * up
        return _qmatmul(fuse, w_down, s_down)
    x = L0_attn_x
    x = _layernorm(x + _L0_attn_ref(x, L0_attn_w_q, L0_attn_w_k, L0_attn_w_v, L0_attn_w_o), axis=-1)
    x = _layernorm(x + _L0_ffn_ref(x, L0_ffn_w_gate, L0_ffn_w_up, L0_ffn_w_down, L0_ffn_s_gate, L0_ffn_s_up, L0_ffn_s_down), axis=-1)
    return x

_drawn_inputs = setup_inputs


def setup_inputs(seed=0):
    import zlib

    import numpy as np

    out = dict(_drawn_inputs(seed))
    spreads = {}
    factors = {}
    for name, (base, spread) in spreads.items():
        noise = np.random.default_rng([zlib.crc32(name.encode()), seed]).standard_normal(out[name].shape)
        drawn = base * np.exp(spread * noise) if base else spread * noise
        out[name] = jnp.asarray(drawn.astype(out[name].dtype))
    for name, factor in factors.items():
        out[name] = (out[name] * factor).astype(out[name].dtype)
    return out
```

```python
from contextlib import ExitStack

import concourse.bass as bass
from concourse import mybir

ALU = mybir.AluOpType
ACT = mybir.ActivationFunctionType
AX_X = mybir.AxisListType.X
F32 = mybir.dt.float32
F32R = mybir.dt.float32r
BF16 = mybir.dt.bfloat16
I8 = mybir.dt.int8
I32 = mybir.dt.int32

P = 128
T = 2048
C = 512
INTER = 2048
HD = 32
KC = C // P
HG = P // HD
G = C // P
BLK = 512
NB = T // BLK
TB = BLK // P
QGRP = 128
SCALE = float(HD) ** -0.5
W_EPS = 1e-8
LN_EPS = 1e-5
LOWEST = -3.0e38
MROW = 3 * HD
NCH = 12
NO = INTER // P




QSTEPS = 4


def quantize_tile(dve, nc, raw, wide, small, step, base, k):
    nc.vector.tensor_reduce(small[:, 0:4], raw.rearrange("p (g c) -> p g c", c=QGRP), AX_X, ALU.add,
                            apply_absolute_value=True).then_inc(step, 1)
    dve.wait_ge(step, base + k + 1)
    nc.vector.tensor_scalar(small[:, 4:8], small[:, 0:4], 1.0 / QGRP, W_EPS, ALU.mult, ALU.max).then_inc(step, 1)
    dve.wait_ge(step, base + k + 2)
    nc.vector.tensor_scalar(small[:, 8:12], small[:, 4:8], 0.5, None, ALU.mult)
    nc.vector.tensor_scalar(small[:, 12:16], small[:, 4:8], -0.5, None, ALU.mult).then_inc(step, 1)
    dve.wait_ge(step, base + k + 3)
    for g in range(C // QGRP):
        cols = slice(g * QGRP, (g + 1) * QGRP)
        nc.vector.tensor_scalar(wide[:, 0, cols], raw[:, cols], small[:, 8 + g:9 + g], small[:, 4 + g:5 + g],
                                ALU.is_gt, ALU.mult)
        last = nc.vector.tensor_scalar(wide[:, 1, cols], raw[:, cols], small[:, 12 + g:13 + g],
                                       small[:, 4 + g:5 + g], ALU.is_lt, ALU.mult)
    last.then_inc(step, 1)
    dve.wait_ge(step, base + k + 4)



def project_program(nc, x, w_qkv, rope, q_all, k_all, v_all, ident):
    NT = 3 * G
    NP = 2 * G + TB
    NR = 2 * G
    with ExitStack() as ctx:
        def sb(name, shape, dt):
            return ctx.enter_context(nc.sbuf_tensor("pj_" + name, shape, dt))

        def sem(name):
            return ctx.enter_context(nc.semaphore("pj_" + name))

        wt_hi = sb("wt_hi", [P, NT, KC, P], F32R)
        wt_lo = sb("wt_lo", [P, NT, KC, P], F32R)
        w_raw = sb("w_raw", [P, 2, C], F32)
        w_q = sb("w_q", [P, 2, 2, C], F32)
        w_small = sb("w_small", [P, 2, 16], F32)
        x_nat = sb("x_nat", [P, TB, C], F32)
        xt_hi = sb("xt_hi", [P, KC, BLK], F32R)
        xt_lo = sb("xt_lo", [P, KC, BLK], F32R)
        rope_t = sb("rope_t", [P, 2, BLK], F32)
        proj = sb("proj", [P, 2, BLK], F32)
        turned = sb("turned", [P, 2, BLK], F32)
        by_cos = sb("by_cos", [P, 2, BLK], F32)
        ps_t = ctx.enter_context(nc.psum_tensor("pj_ps_t", [P, KC, BLK], F32))
        ps_o = ctx.enter_context(nc.psum_tensor("pj_ps_o", [P, 4, BLK], F32))

        ident_zero, ident_ready = sem("ident_zero"), sem("ident_ready")
        w_loaded = [sem("w_loaded0"), sem("w_loaded1")]
        w_step, w_signs, w_sub, w_ste = sem("w_step"), sem("w_signs"), sem("w_sub"), sem("w_ste")
        w_turned, w_hi_done, w_lo_done = sem("w_turned"), sem("w_hi_done"), sem("w_lo_done")
        x_loaded, rope_loaded, passed = sem("x_loaded"), sem("rope_loaded"), sem("passed")
        x_turned, x_hi_done, x_lo_done = sem("x_turned"), sem("x_hi_done"), sem("x_lo_done")
        prod_ready, prod_copied = sem("prod_ready"), sem("prod_copied")
        turn_done, cos_done, sin_done, rope_done = sem("turn_done"), sem("cos_done"), sem("sin_done"), sem("rope_done")
        W2, KC4, O4, R2 = 2, KC, 4, 2

        with nc.Block() as block:
            @block.sync
            def _(sp):
                with sp.Fori(0, NT // 2) as i:
                    for j in range(2):
                        sp.wait_ge(w_ste, i * 2 + (j + 1))
                        sp.dma_start(w_raw[:, j, :], w_qkv[i * 2 + j]).then_inc(w_loaded[j], 16)
                with sp.Fori(0, NB) as b:
                    sp.wait_ge(x_turned, b * KC + KC4)
                    sp.dma_start(x_nat[:], x[b]).then_inc(x_loaded, 16)
                    sp.wait_ge(rope_done, b * NR + R2)
                    for q in range(HG):
                        sp.dma_start(rope_t[q * HD:(q + 1) * HD, :, :], rope[b]).then_inc(rope_loaded, 16)

            @block.gpsimd
            def _(pool):
                pool.sem_inc(w_ste, W2)
                nc.gpsimd.memset(ident[:], 0.0).then_inc(ident_zero, 1)
                pool.wait_ge(ident_zero, 1)
                nc.gpsimd.affine_select(out=ident[:], in_=ident[:], compare_op=ALU.not_equal, fill=1.0, base=0,
                                        pattern=[[-1, P]], channel_multiplier=1).then_inc(ident_ready, 1)
                with pool.Fori(0, NT // 2) as i:
                    for j in range(2):
                        pool.wait_ge(w_signs, i * 2 + (j + 1))
                        nc.gpsimd.tensor_tensor(w_q[:, j, 1, :], w_q[:, j, 0, :], w_raw[:, j, :],
                                                ALU.subtract).then_inc(w_sub, 1)
                        pool.wait_ge(w_sub, i * 2 + (j + 1))
                        nc.gpsimd.tensor_tensor(w_q[:, j, 0, :], w_raw[:, j, :], w_q[:, j, 1, :],
                                                ALU.add).then_inc(w_ste, 1)
                with pool.Fori(0, NB) as b:
                    pool.wait_ge(rope_loaded, b * (16 * HG) + 16 * HG)
                    for i in range(NR):
                        pool.wait_ge(prod_copied, b * NP + (O4 + i + 1))
                        pool.wait_ge(rope_done, b * NR + (i + 1))
                        nc.gpsimd.tensor_tensor(by_cos[:, i % 2, :], proj[:, i % 2, :], rope_t[:, 0, :],
                                                ALU.mult).then_inc(cos_done, 1)

            @block.tensor
            def _(pe):
                pe.sem_inc(w_turned, W2)
                pe.sem_inc(x_turned, KC4)
                pe.wait_ge(ident_ready, 1)
                with pe.Fori(0, NT // 2) as i:
                    for j in range(2):
                        pe.wait_ge(w_ste, i * 2 + (W2 + j + 1))
                        pe.wait_ge(w_lo_done, i * 2 + (j + 1))
                        for k in range(KC):
                            last = nc.tensor.transpose(ps_t[:, j, k * P:(k + 1) * P],
                                                       w_q[:, j, 0, k * P:(k + 1) * P], ident[:])
                        last.then_inc(w_turned, 1)
                pe.wait_ge(w_lo_done, NT + W2)
                with pe.Fori(0, NB) as b:
                    pe.wait_ge(x_loaded, b * 16 + 16)
                    for k in range(KC):
                        pe.wait_ge(x_lo_done, b * KC + (k + 1))
                        for t in range(TB):
                            last = nc.tensor.transpose(ps_t[:, k, t * P:(t + 1) * P],
                                                       x_nat[:, t, k * P:(k + 1) * P], ident[:])
                        last.then_inc(x_turned, 1)
                    for i in range(NP):
                        pe.wait_ge(prod_copied, b * NP + (i + 1))
                        if i < NR:
                            terms = [(wt_hi, xt_hi), (wt_hi, xt_lo), (wt_lo, xt_hi)]
                        else:
                            terms = [(xt_hi, wt_hi), (xt_lo, wt_hi), (xt_hi, wt_lo)]
                        for n, (w, m) in enumerate(terms):
                            for k in range(KC):
                                if i == 0 and n < 2:
                                    part_done = (x_hi_done, x_lo_done)[n]
                                    pe.wait_ge(part_done, b * KC + ((KC4 if n == 1 else 0) + k + 1))
                                if i < NR:
                                    lhs, rhs = w[:, i, k, :], m[:, k, :]
                                else:
                                    lhs, rhs = w[:, k, (i - NR) * P:(i - NR + 1) * P], m[:, 2 * G:3 * G, k, :]
                                last = nc.tensor.matmul(ps_o[:, i % 4, :], lhs, rhs,
                                                        start=(n == 0 and k == 0), stop=(n == 2 and k == KC - 1))
                        last.then_inc(prod_ready, 1)

            @block.scalar
            def _(act):
                act.sem_inc(prod_copied, O4)
                with act.Fori(0, NT // 2) as i:
                    for j in range(2):
                        act.wait_ge(w_turned, i * 2 + (W2 + j + 1))
                        nc.scalar.activation(wt_hi[:, i * 2 + j, :, :],
                                             ps_t[:, j, :].rearrange("p (k c) -> p k c", c=P),
                                             ACT.Copy).then_inc(w_hi_done, 1)
                with act.Fori(0, NB) as b:
                    for k in range(KC):
                        act.wait_ge(x_turned, b * KC + (KC4 + k + 1))
                        nc.scalar.activation(xt_hi[:, k, :], ps_t[:, k, :], ACT.Copy).then_inc(x_hi_done, 1)
                    for i in range(NP):
                        act.wait_ge(prod_ready, b * NP + (i + 1))
                        if i < NR:
                            act.wait_ge(rope_done, b * NR + (i + 1))
                            nc.scalar.activation(proj[:, i % 2, :], ps_o[:, i % 4, :],
                                                 ACT.Copy).then_inc(prod_copied, 1)
                        else:
                            nc.scalar.activation(v_all[:, b * TB + (i - NR), :], ps_o[:, i % 4, :],
                                                 ACT.Copy).then_inc(prod_copied, 1)

            @block.vector
            def _(dve):
                dve.sem_inc(w_lo_done, W2)
                dve.sem_inc(x_lo_done, KC4)
                dve.sem_inc(rope_done, R2)
                STEPS = 2 * QSTEPS
                with dve.Fori(0, NT // 2) as i:
                    for j in range(2):
                        dve.wait_ge(w_loaded[j], i * 16 + 16)
                        dve.wait_ge(w_turned, i * 2 + (j + 1))
                        quantize_tile(dve, nc, w_raw[:, j, :], w_q[:, j], w_small[:, j], w_step, i * STEPS, j * QSTEPS)
                        nc.vector.tensor_tensor(w_q[:, j, 0, :], w_q[:, j, 0, :], w_q[:, j, 1, :],
                                                ALU.subtract).then_inc(w_signs, 1)
                    for j in range(2):
                        dve.wait_ge(w_hi_done, i * 2 + (j + 1))
                        nc.vector.tensor_tensor(wt_lo[:, i * 2 + j, :, :],
                                                ps_t[:, j, :].rearrange("p (k c) -> p k c", c=P),
                                                wt_hi[:, i * 2 + j, :, :].bitcast(F32), ALU.subtract).then_inc(w_lo_done, 1)
                swap = [(r + HD // 2) % HD for r in range(HD)]
                with dve.Fori(0, NB) as b:
                    for k in range(KC):
                        dve.wait_ge(x_hi_done, b * KC + (k + 1))
                        nc.vector.tensor_tensor(xt_lo[:, k, :], ps_t[:, k, :], xt_hi[:, k, :].bitcast(F32),
                                                ALU.subtract).then_inc(x_lo_done, 1)
                    dve.wait_ge(rope_loaded, b * (16 * HG) + 16 * HG)
                    for i in range(NR):
                        dst = (q_all if i < G else k_all)[:, i % G, bass.ds(b * BLK, BLK)]
                        dve.wait_ge(prod_copied, b * NP + (O4 + i + 1))
                        dve.sem_inc(passed, 1)
                        nc.vector.stream_shuffle(turned[:, i % 2, :], proj[:, i % 2, :], swap).then_inc(turn_done, 1)
                        dve.wait_ge(turn_done, b * NR + (i + 1))
                        nc.vector.tensor_tensor(turned[:, i % 2, :], turned[:, i % 2, :], rope_t[:, 1, :],
                                                ALU.mult).then_inc(sin_done, 1)
                        dve.wait_ge(sin_done, b * NR + (i + 1))
                        dve.wait_ge(cos_done, b * NR + (i + 1))
                        nc.vector.tensor_tensor(dst, by_cos[:, i % 2, :], turned[:, i % 2, :],
                                                ALU.add).then_inc(rope_done, 1)


AU = [16 * (b + 1) for b in range(NB)]
KT = [TB * (b + 1) for b in range(NB)]
NA, NK = sum(AU), sum(KT)


def units(b):
    return [(j, qt, c) for c in range(b + 1) for qt in range(TB) for j in range(HG)]


def interleave(b, parts, first):
    gaps, order = [], []
    for i in range(KT[b]):
        items = [("scores", i, 0), ("scores", i, 1)]
        if i:
            items += [("values", i - 1), ("sums", i - 1)]
        for it in items:
            order.append([it])
            if i >= first:
                gaps.append(order[-1])
    if parts:
        for u in range(parts):
            gaps[u * len(gaps) // parts].append(("max", u))
        order.append([("maxima",)])
    order.append([("values", KT[b] - 1), ("sums", KT[b] - 1)])
    return [it for group in order for it in group]


def steps(last):
    out = []
    for b in range(NB):
        m = b + 1 if b + 1 < NB else (None if last else 0)
        out.append((b, m, interleave(b, AU[m] if m is not None else 0, 0 if b + 1 < NB else TB + 2)))
    return out


def attention_program(nc, q_all, k_all, v_all, ident):
    with ExitStack() as ctx:
        def sb(name, shape, dt):
            return ctx.enter_context(nc.sbuf_tensor("at_" + name, shape, dt))

        def sem(name):
            return ctx.enter_context(nc.semaphore("at_" + name))

        k_stack = sb("k_stack", [P, HG, T], F32R)
        q_stack = sb("q_stack", [P, 2, HG, BLK], F32R)
        v_grp = sb("v_grp", [P, T // P, P], F32)
        k_part = sb("k_part", [P, 2, 2, BLK], F32R)
        q_part = sb("q_part", [P, 2, 2, BLK], F32R)
        probs = sb("probs", [P, 2, HG, BLK], F32)
        tail = sb("tail", [P, HG], F32)
        strip = sb("strip", [P, BLK], F32)
        spill = sb("spill", [P, 2, BLK], BF16)
        ones = sb("ones", [P, HD], F32)
        part_max = sb("part_max", [P, 2, TB * HG, NB], F32)
        neg_max = sb("neg_max", [P, 2, TB * HG], F32)
        neg_max_hi = sb("neg_max_hi", [P, 2, TB * HG], F32R)
        turn_in = sb("turn_in", [P, 2, TB, P], F32)
        inv_sum = sb("inv_sum", [P, BLK], F32)
        ps_m = ctx.enter_context(nc.psum_tensor("at_ps_m", [P, 2, BLK], F32))
        ps_s = ctx.enter_context(nc.psum_tensor("at_ps_s", [P, HG, BLK], F32))
        ps_y = ctx.enter_context(nc.psum_tensor("at_ps_y", [P, BLK], F32))
        ps_l = ctx.enter_context(nc.psum_tensor("at_ps_l", [P, BLK], F32))

        const_step, consts_ready = sem("const_step"), sem("consts_ready")
        split_hi, split_done = sem("split_hi"), sem("split_done")
        staged = [sem("staged0"), sem("staged1")]
        unit_ready, unit_drained = sem("unit_ready"), sem("unit_drained")
        max_step, max_ready, max_turned, max_placed = (
            sem("max_step"), sem("max_ready"), sem("max_turned"), sem("max_placed"))
        scores_ready, exp_done, masked, values_done = (
            sem("scores_ready"), sem("exp_done"), sem("masked"), sem("values_done"))
        inv_done, norm_done, passed = sem("inv_done"), sem("norm_done"), sem("passed")
        BATCH = 16 * (6 * HG + 1)
        V2, N1 = 2, 1

        cum_u = [sum(AU[:b]) for b in range(NB + 1)]
        cum_k = [sum(KT[:b]) for b in range(NB + 1)]
        SPLITS = 4

        def passes(eng, body):
            with eng.Fori(0, G - 1) as g:
                body(g, False)
            body(G - 1, True)

        with nc.Block() as block:
            @block.gpsimd
            def _(pool):
                def split(g, b, n):
                    for src, dst in ((k_all, k_part), (q_all, q_part)):
                        nc.gpsimd.tensor_copy(dst[:, b % 2, 0, :], src[:, g, b * BLK:(b + 1) * BLK]).then_inc(split_hi, 1)
                    for m, (src, dst) in enumerate(((k_all, k_part), (q_all, q_part))):
                        pool.wait_ge(split_hi, n * 2 + (m + 1))
                        pool.sem_inc(passed, 1)
                        nc.gpsimd.tensor_tensor(dst[:, b % 2, 1, :], src[:, g, b * BLK:(b + 1) * BLK],
                                                dst[:, b % 2, 0, :].bitcast(F32), ALU.subtract).then_inc(split_done, 1)

                nc.gpsimd.memset(tail[:], 0.0).then_inc(const_step, 1)
                nc.gpsimd.memset(strip[:], 0.0).then_inc(const_step, 1)
                nc.gpsimd.memset(turn_in[:], 0.0).then_inc(consts_ready, 1)
                nc.gpsimd.memset(ones[:], 1.0).then_inc(consts_ready, 1)
                pool.wait_ge(const_step, 2)
                nc.gpsimd.affine_select(out=strip[:], in_=strip[:], compare_op=ALU.is_ge, fill=LOWEST, base=BLK - P,
                                        pattern=[[-1, BLK]], channel_multiplier=1).then_inc(consts_ready, 1)
                for r in range(2):
                    nc.gpsimd.affine_select(out=tail[:], in_=tail[:], compare_op=ALU.not_equal, fill=1.0,
                                            base=-MROW - r, pattern=[[-2, HG]], channel_multiplier=1).then_inc(const_step, 1)
                    pool.wait_ge(const_step, 3 + r)
                split(0, 0, 0)
                split(0, 1, 1)

                def body(g, last):
                    for b, m, order in steps(last):
                        for it in order:
                            if it[0] == "scores" and it[1] >= KT[b] - TB:
                                d = it[1] - (KT[b] - TB)
                                pool.wait_ge(exp_done, g * (2 * NK) + (2 * (cum_k[b] + it[1]) + it[2] + 1))
                                tri = probs[:, (cum_k[b] + it[1]) % 2, 2 * it[2]:2 * it[2] + 2, d * P:(d + 1) * P]
                                pool.sem_inc(passed, 1)
                                nc.gpsimd.affine_select(out=tri, in_=tri, compare_op=ALU.is_ge, fill=0.0, base=0,
                                                        pattern=[[0, 2], [1, P]], channel_multiplier=-1).then_inc(masked, 1)
                            if it == ("scores", KT[b] - TB - 1, 1) or (b == 0 and it == ("scores", TB - 1, 1)):
                                nxt = b + 2
                                gg, bb = (g, nxt) if nxt < NB else (g + 1, nxt - NB)
                                if gg is g or not last:
                                    pool.wait_ge(staged[bb % 2], g * (2 * BATCH) + BATCH * (1 + (b // 2)))
                                    split(gg, bb, g * NB + (b + 2))
                passes(pool, body)

            @block.sync
            def _(sp):
                def stage(g, b, n):
                    sp.wait_ge(split_done, n * 2 + 2)
                    done = staged[b % 2]
                    cols = slice(b * BLK, (b + 1) * BLK)
                    for j in range(HG):
                        rows = slice(j * HD, (j + 1) * HD)
                        for r, (kp, qp) in enumerate(((0, 0), (1, 0), (0, 1))):
                            at = slice(r * HD, (r + 1) * HD)
                            sp.dma_start(q_stack[at, b % 2, j, :].bitcast(F32), q_part[rows, b % 2, qp, :].bitcast(F32)).then_inc(done, 16)
                            sp.dma_start(k_stack[at, j, cols].bitcast(F32), k_part[rows, b % 2, kp, :].bitcast(F32)).then_inc(done, 16)
                    sp.dma_start(v_grp[:, b * TB:(b + 1) * TB, :],
                                 v_all[:, b * TB:(b + 1) * TB, bass.ds(g * P, P)]).then_inc(done, 16)

                stage(0, 0, 0)
                stage(0, 1, 1)

                def body(g, last):
                    sp.wait_ge(values_done, g * NK + (V2 + cum_k[1]))
                    stage(g, 2, g * NB + 2)
                    sp.wait_ge(values_done, g * NK + (V2 + cum_k[2]))
                    stage(g, 3, g * NB + 3)
                    if not last:
                        sp.wait_ge(values_done, g * NK + (V2 + cum_k[3] + TB))
                        stage(g + 1, 0, g * NB + 4)
                        sp.wait_ge(values_done, g * NK + (V2 + cum_k[4]))
                        stage(g + 1, 1, g * NB + 5)
                passes(sp, body)

            @block.tensor
            def _(pe):
                pe.sem_inc(values_done, V2)
                pe.wait_ge(consts_ready, 4)
                ring = []

                def unit(g, b, u, base_u):
                    j, qt, c = units(b)[u]
                    n = len(ring)
                    if n >= 2:
                        wait_bank(g, ring[n - 2])
                    w = BLK if c < b else (qt + 1) * P
                    nc.tensor.matmul(ps_m[:, (ring_start + n) % 2, 0:w],
                                     q_stack[0:MROW, b % 2, j, qt * P:(qt + 1) * P],
                                     k_stack[0:MROW, j, c * BLK:c * BLK + w], start=True, stop=True).then_inc(unit_ready, 1)
                    ring.append((unit_drained, base_u + u + 1))

                def wait_bank(g, use):
                    s, v = use
                    per = NA if s is unit_drained else NB
                    pe.wait_ge(s, g * per + v)

                def turn_maxima(g, b, n):
                    r = len(ring)
                    wait_bank(g, ring[r - 2])
                    pe.wait_ge(max_ready, g * NB + n)
                    for qt in range(TB):
                        last = nc.tensor.transpose(ps_m[:, (ring_start + r) % 2, qt * P:(qt + 1) * P],
                                                   turn_in[:, b % 2, qt, :], ident[:])
                    last.then_inc(max_turned, 1)
                    ring.append((max_placed, n))

                ring_start = 0
                pe.wait_ge(staged[0], BATCH)
                for u in range(AU[0]):
                    unit(0, 0, u, 0)
                turn_maxima(0, 0, 1)
                ring_start = len(ring)

                def body(g, last):
                    del ring[:]
                    base_u = AU[0]
                    for b, m, order in steps(last):
                        off = lambda i: max(0, i - (KT[b] - TB)) * P
                        placed = False
                        unit_seen = False
                        for it in order:
                            if it[0] == "scores":
                                i, pair = it[1], it[2]
                                kt = cum_k[b] + i
                                if not placed:
                                    pe.wait_ge(max_placed, g * NB + (b + 1))
                                    placed = True
                                if kt >= 1:
                                    pe.wait_ge(exp_done, g * (2 * NK) + (2 * (kt - 1) + pair + 1))
                                for j in (2 * pair, 2 * pair + 1):
                                    last_mm = nc.tensor.matmul(ps_s[:, j, off(i):BLK], k_stack[:, j, i * P:(i + 1) * P],
                                                               q_stack[:, b % 2, j, off(i):BLK], start=True, stop=True)
                                last_mm.then_inc(scores_ready, 1)
                            elif it[0] == "values":
                                i = it[1]
                                kt = cum_k[b] + i
                                if i == 0:
                                    pe.wait_ge(norm_done, g * NB + (N1 + b))
                                if i >= KT[b] - TB:
                                    pe.wait_ge(masked, g * (2 * TB * NB) + 2 * (TB * b + i - (KT[b] - TB) + 1))
                                else:
                                    pe.wait_ge(exp_done, g * (2 * NK) + 2 * (kt + 1))
                                for j in range(HG):
                                    nc.tensor.matmul(ps_y[j * HD:(j + 1) * HD, off(i):BLK], v_grp[:, i, j * HD:(j + 1) * HD],
                                                     probs[:, kt % 2, j, off(i):BLK], start=(i == 0), stop=(i == KT[b] - 1),
                                                     )
                            elif it[0] == "sums":
                                i = it[1]
                                kt = cum_k[b] + i
                                for j in range(HG):
                                    last_mm = nc.tensor.matmul(ps_l[j * HD:(j + 1) * HD, off(i):BLK], ones[:, :],
                                                               probs[:, kt % 2, j, off(i):BLK], start=(i == 0),
                                                               stop=(i == KT[b] - 1))
                                last_mm.then_inc(values_done, 1)
                            elif it[0] == "max":
                                if not unit_seen:
                                    pe.wait_ge(staged[m % 2], g * (2 * BATCH) + BATCH * {1: 1, 2: 2, 3: 2, 0: 3}[m])
                                    unit_seen = True
                                unit(g, m, it[1], base_u)
                            else:
                                turn_maxima(g, m, b + 2)
                                base_u += AU[m]
                passes(pe, body)

            @block.scalar
            def _(act):
                def place_maxima(g, b, n, r):
                    act.wait_ge(max_turned, g * NB + n)
                    nc.scalar.activation(q_stack[MROW:P, b % 2, :, :],
                                         ps_m[MROW:P, r % 2, :].unsqueeze(1).to_broadcast([P - MROW, HG, BLK]),
                                         ACT.Copy).then_inc(max_placed, 1)

                place_maxima(0, 0, 1, AU[0])

                def body(g, last):
                    r = AU[0] + 1
                    for b, m, order in steps(last):
                        for it in order:
                            if it[0] == "scores":
                                i, pair = it[1], it[2]
                                kt = cum_k[b] + i
                                lo = max(0, i - (KT[b] - TB)) * P
                                act.wait_ge(scores_ready, g * (2 * NK) + (2 * kt + pair + 1))
                                act.wait_ge(values_done, g * NK + (kt + 1))
                                nc.scalar.activation(probs[:, kt % 2, 2 * pair:2 * pair + 2, lo:BLK],
                                                     ps_s[:, 2 * pair:2 * pair + 2, lo:BLK], ACT.Exp,
                                                     scale=SCALE).then_inc(exp_done, 1)
                            elif it[0] == "maxima":
                                r += AU[m]
                                place_maxima(g, m, b + 2, r)
                                r += 1
                passes(act, body)

            @block.vector
            def _(dve):
                dve.sem_inc(norm_done, N1)
                dve.wait_ge(const_step, 4)
                nc.vector.tensor_copy(k_stack[MROW:P, :, :],
                                      tail[MROW:P, :].unsqueeze(2).to_broadcast([P - MROW, HG, T])).then_inc(consts_ready, 1)
                dve.wait_ge(consts_ready, 4)

                def drain_unit(g, b, u, base_u, r, spilled):
                    j, qt, c = units(b)[u]
                    dve.wait_ge(unit_ready, g * NA + (base_u + u + 1))
                    out = part_max[:, b % 2, qt * HG + j, c:c + 1]
                    if c < b:
                        nc.vector.tensor_reduce(out, ps_m[:, r % 2, :], AX_X, ALU.max).then_inc(unit_drained, 1)
                    else:
                        w = (qt + 1) * P
                        if len(spilled) >= 2:
                            dve.wait_ge(unit_drained, g * NA + spilled[-2])
                        dve.sem_inc(passed, 1)
                        nc.vector.tensor_tensor_reduce(spill[:, len(spilled) % 2, 0:w], ps_m[:, r % 2, 0:w],
                                                       strip[:, BLK - w:BLK], 1.0, LOWEST, ALU.add, ALU.max,
                                                       out).then_inc(unit_drained, 1)
                        spilled.append(base_u + u + 1)

                def finish_maxima(g, b, n, base_u):
                    buf = b % 2
                    dve.wait_ge(unit_drained, g * NA + (base_u + AU[b]))
                    nc.vector.tensor_reduce(neg_max[:, buf, :], part_max[:, buf, :, 0:b + 1], AX_X, ALU.max,
                                            negate=True).then_inc(max_step, 1)
                    dve.wait_ge(max_step, g * (2 * NB) + (2 * n - 1))
                    nc.vector.tensor_copy(neg_max_hi[:, buf, :], neg_max[:, buf, :]).then_inc(max_step, 1)
                    dve.wait_ge(max_step, g * (2 * NB) + 2 * n)
                    to = turn_in[:, buf, :, MROW:MROW + 2 * HG].rearrange("p t (j r) -> p t j r", r=2)
                    hi = neg_max_hi[:, buf, :].bitcast(F32).rearrange("p (t j) -> p t j", j=HG)
                    nc.vector.tensor_copy(to[:, :, :, 0], hi)
                    nc.vector.tensor_tensor(to[:, :, :, 1], neg_max[:, buf, :].rearrange("p (t j) -> p t j", j=HG), hi,
                                            ALU.subtract).then_inc(max_ready, 1)

                def normalise(g, b):
                    dve.wait_ge(values_done, g * NK + (V2 + cum_k[b + 1]))
                    nc.vector.reciprocal(inv_sum[:], ps_l[:]).then_inc(inv_done, 1)
                    dve.wait_ge(inv_done, g * NB + (b + 1))
                    nc.vector.tensor_tensor(q_all[:, g, b * BLK:(b + 1) * BLK], ps_y[:], inv_sum[:],
                                            ALU.mult).then_inc(norm_done, 1)

                spilled = []
                for u in range(AU[0]):
                    drain_unit(0, 0, u, 0, u, spilled)
                finish_maxima(0, 0, 1, 0)

                def body(g, last):
                    r, base_u, spilled = AU[0] + 1, AU[0], []
                    for b, m, order in steps(last):
                        if b >= 1:
                            normalise(g, b - 1)
                        for it in order:
                            if it[0] == "max":
                                drain_unit(g, m, it[1], base_u, r, spilled)
                                r += 1
                            elif it[0] == "maxima":
                                finish_maxima(g, m, b + 2, base_u)
                                r += 1
                                base_u += AU[m]
                    normalise(g, NB - 1)
                passes(dve, body)


def output_program(nc, x, w_o, w_ffn, y_all, x1_all, w_ffn_sb, ident):
    TT = T // P
    with ExitStack() as ctx:
        def sb(name, shape, dt):
            return ctx.enter_context(nc.sbuf_tensor("op_" + name, shape, dt))

        def sem(name):
            return ctx.enter_context(nc.semaphore("op_" + name))

        wo_hi = sb("wo_hi", [P, KC, C], F32R)
        wo_lo = sb("wo_lo", [P, KC, C], F32R)
        w_raw = sb("w_raw", [P, 2, C], F32)
        w_q = sb("w_q", [P, 2, 2, C], F32)
        w_small = sb("w_small", [P, 2, 16], F32)
        w_i8 = sb("w_i8", [P, 2, INTER // 4], I32)
        y_hi = sb("y_hi", [P, 2, KC, P], F32R)
        y_lo = sb("y_lo", [P, 2, KC, P], F32R)
        x_in = sb("x_in", [P, 2, C], F32)
        res = w_raw
        stats = sb("stats", [P, 2, 6], F32)
        mean_var = sb("mean_var", [P, 2, 2], F32)
        var_eps = sb("var_eps", [P, 2], F32)
        rstd = sb("rstd", [P, 2], F32)
        half = sb("half", [P, 1], F32)
        ps_t = ctx.enter_context(nc.psum_tensor("op_ps_t", [P, 2, C], F32))
        ps_o = ctx.enter_context(nc.psum_tensor("op_ps_o", [P, 2, C], F32))

        w_loaded = [sem("wo_loaded0"), sem("wo_loaded1")]
        w_step, w_signs, w_sub, w_ste = sem("wo_step"), sem("wo_signs"), sem("wo_sub"), sem("wo_ste")
        w_turned, w_hi_done, w_lo_done = sem("wo_turned"), sem("wo_hi_done"), sem("wo_lo_done")
        ffn_loaded, ffn_done = [sem("ffn_loaded0"), sem("ffn_loaded1")], sem("ffn_done")
        x_loaded = [sem("xin_loaded0"), sem("xin_loaded1")]
        half_set, passed = sem("half_set"), sem("passed")
        y_hi_done, y_lo_done, out_ready = sem("y_hi_done"), sem("y_lo_done"), sem("out_ready")
        res_done, stats_done, var_done, rstd_done, x1_done = (
            sem("res_done"), sem("stats_done"), sem("var_done"), sem("rstd_done"), sem("x1_done"))
        B2 = 2

        with nc.Block() as block:
            @block.sync
            def _(sp):
                for j in range(KC):
                    if j >= 2:
                        sp.wait_ge(w_ste, j - 1)
                    sp.dma_start(w_raw[:, j % 2, :], w_o[j]).then_inc(w_loaded[j % 2], 16)
                with sp.Fori(0, NCH // 2) as i:
                    for j in range(2):
                        sp.wait_ge(res_done, i * 2 + (j + 1))
                        sp.dma_start(x_in[:, j, :], x[i * 2 + j]).then_inc(x_loaded[j], 16)
                        sp.wait_ge(ffn_done, i * 2 + (j + 1))
                        sp.dma_start(w_i8[:, j, :], w_ffn[i * 2 + j]).then_inc(ffn_loaded[j], 16)
                with sp.Fori(NCH // 2, TT // 2) as i:
                    for j in range(2):
                        sp.wait_ge(res_done, i * 2 + (j + 1))
                        sp.dma_start(x_in[:, j, :], x[i * 2 + j]).then_inc(x_loaded[j], 16)

            @block.gpsimd
            def _(pool):
                nc.gpsimd.memset(half[:], -0.5).then_inc(half_set, 1)
                for j in range(KC):
                    pool.wait_ge(w_signs, j + 1)
                    nc.gpsimd.tensor_tensor(w_q[:, j % 2, 1, :], w_q[:, j % 2, 0, :], w_raw[:, j % 2, :],
                                            ALU.subtract).then_inc(w_sub, 1)
                    pool.wait_ge(w_sub, j + 1)
                    nc.gpsimd.tensor_tensor(w_q[:, j % 2, 0, :], w_raw[:, j % 2, :], w_q[:, j % 2, 1, :],
                                            ALU.add).then_inc(w_ste, 1)
                pool.wait_ge(half_set, 1)
                with pool.Fori(0, TT // 2) as i:
                    for j in range(2):
                        pool.wait_ge(var_done, i * 2 + (j + 1))
                        nc.gpsimd.tensor_tensor(rstd[:, j:j + 1], var_eps[:, j:j + 1], half[:], ALU.pow).then_inc(rstd_done, 1)

            @block.tensor
            def _(pe):
                pe.sem_inc(out_ready, B2)
                for j in range(KC):
                    pe.wait_ge(w_ste, j + 1)
                    if j >= 2:
                        pe.wait_ge(w_lo_done, j - 1)
                    for k in range(KC):
                        last = nc.tensor.transpose(ps_t[:, j % 2, k * P:(k + 1) * P],
                                                   w_q[:, j % 2, 0, k * P:(k + 1) * P], ident[:])
                    last.then_inc(w_turned, 1)
                pe.wait_ge(w_lo_done, KC)
                with pe.Fori(0, TT // 2) as i:
                    for j in range(2):
                        pe.wait_ge(res_done, i * 2 + (j + 1))
                        pe.wait_ge(y_hi_done, i * 2 + (j + 1))
                        for n, (y, w) in enumerate(((y_hi, wo_hi), (y_hi, wo_lo), (y_lo, wo_hi))):
                            if n == 2:
                                pe.wait_ge(y_lo_done, i * 2 + (j + 1))
                            for k in range(KC):
                                last = nc.tensor.matmul(ps_o[:, j, :], y[:, j, k, :], w[:, k, :],
                                                        start=(n == 0 and k == 0), stop=(n == 2 and k == KC - 1))
                        last.then_inc(out_ready, 1)

            @block.scalar
            def _(act):
                act.sem_inc(ffn_done, B2)
                for j in range(KC):
                    act.wait_ge(w_turned, j + 1)
                    nc.scalar.activation(wo_hi[:, :, j * P:(j + 1) * P], ps_t[:, j % 2, :].rearrange("p (k c) -> p k c", c=P),
                                         ACT.Copy).then_inc(w_hi_done, 1)
                with act.Fori(0, NCH // 2) as i:
                    for j in range(2):
                        act.wait_ge(out_ready, i * 2 + (j + 1))
                        nc.scalar.activation(y_hi[:, j, :, :], y_all[:, :, bass.ds((i * 2 + j) * P, P)],
                                             ACT.Copy).then_inc(y_hi_done, 1)
                        act.wait_ge(ffn_loaded[j], i * 16 + 16)
                        nc.scalar.activation(w_ffn_sb[:, i * 2 + j, :], w_i8[:, j, :].bitcast(I8), ACT.Copy).then_inc(ffn_done, 1)
                for t in range(NCH, TT):
                    act.wait_ge(out_ready, t + 1)
                    nc.scalar.activation(y_hi[:, t % 2, :, :], y_all[:, :, t * P:(t + 1) * P],
                                         ACT.Copy).then_inc(y_hi_done, 1)

            @block.vector
            def _(dve):
                dve.sem_inc(res_done, B2)
                dve.sem_inc(x1_done, B2)
                for j in range(KC):
                    dve.wait_ge(w_loaded[j % 2], 16 * (j // 2 + 1))
                    if j >= 2:
                        dve.wait_ge(w_turned, j - 1)
                    quantize_tile(dve, nc, w_raw[:, j % 2, :], w_q[:, j % 2], w_small[:, j % 2], w_step, 0, j * QSTEPS)
                    nc.vector.tensor_tensor(w_q[:, j % 2, 0, :], w_q[:, j % 2, 0, :], w_q[:, j % 2, 1, :],
                                            ALU.subtract).then_inc(w_signs, 1)
                    dve.wait_ge(w_hi_done, j + 1)
                    nc.vector.tensor_tensor(wo_lo[:, :, j * P:(j + 1) * P], ps_t[:, j % 2, :].rearrange("p (k c) -> p k c", c=P),
                                            wo_hi[:, :, j * P:(j + 1) * P].bitcast(F32), ALU.subtract).then_inc(w_lo_done, 1)
                with dve.Fori(0, TT // 2) as i:
                    for j in range(2):
                        dve.wait_ge(y_hi_done, i * 2 + (j + 1))
                        nc.vector.tensor_tensor(y_lo[:, j, :, :], y_all[:, :, bass.ds((i * 2 + j) * P, P)],
                                                y_hi[:, j, :, :].bitcast(F32), ALU.subtract).then_inc(y_lo_done, 1)
                    for j in range(2):
                        n = i * 2
                        dve.wait_ge(x_loaded[j], i * 16 + 16)
                        dve.wait_ge(out_ready, n + (B2 + j + 1))
                        dve.wait_ge(x1_done, n + (j + 1))
                        nc.vector.tensor_tensor(res[:, j, :], ps_o[:, j, :], x_in[:, j, :], ALU.add).then_inc(res_done, 1)
                        dve.wait_ge(res_done, n + (B2 + j + 1))
                        nc.vector.bn_stats(stats[:, j, :], res[:, j, :]).then_inc(stats_done, 1)
                        dve.wait_ge(stats_done, n * 2 + (2 * j + 1))
                        dve.sem_inc(passed, 1)
                        nc.vector.bn_aggr(mean_var[:, j, :], stats[:, j, :]).then_inc(stats_done, 1)
                        dve.wait_ge(stats_done, n * 2 + (2 * j + 2))
                        nc.vector.tensor_scalar(var_eps[:, j:j + 1], mean_var[:, j, 1:2], LN_EPS, None,
                                                ALU.add).then_inc(var_done, 1)
                    for j in range(2):
                        dve.wait_ge(rstd_done, i * 2 + (j + 1))
                        nc.vector.tensor_scalar(x1_all[:, i * 2 + j, :], res[:, j, :], mean_var[:, j, 0:1], rstd[:, j:j + 1],
                                                ALU.subtract, ALU.mult).then_inc(x1_done, 1)


def ffn_program(nc, scales, s_down, out, x1_all, w_ffn_sb, ident, spare):
    with ExitStack() as ctx:
        def sb(name, shape, dt):
            return ctx.enter_context(nc.sbuf_tensor("ff_" + name, shape, dt))

        def sem(name):
            return ctx.enter_context(nc.semaphore("ff_" + name))

        s_gu = sb("s_gu", [P, 2, NO], F32)
        s_dn = sb("s_dn", [P, C], F32)
        x1_blk = spare[:, 0, :].rearrange("p (t c) -> p t c", c=C)
        x1t_hi = sb("x1t_hi", [P, KC, BLK], F32R)
        x1t_lo = sb("x1t_lo", [P, KC, BLK], F32R)
        gate = sb("gate", [P, 2, BLK], F32)
        fuse = sb("fuse", [P, 2, BLK], F32)
        fuse_hi = sb("fuse_hi", [P, 2, BLK], F32R)
        fuse_lo = sb("fuse_lo", [P, 2, BLK], F32R)
        z = spare[:, 1, :].rearrange("p (t c) -> p t c", c=C)
        result = spare[:, 2, :].rearrange("p (t c) -> p t c", c=C)
        stats = sb("stats2", [P, TB, 6], F32)
        mean_var = sb("mean_var2", [P, TB, 2], F32)
        var_eps = sb("var_eps2", [P, TB], F32)
        rstd = sb("rstd2", [P, TB], F32)
        half = sb("half2", [P, TB], F32)
        ps_g = ctx.enter_context(nc.psum_tensor("ff_ps_g", [P, 2, BLK], F32))
        ps_u = ctx.enter_context(nc.psum_tensor("ff_ps_u", [P, 2, BLK], F32))
        ps_d = ctx.enter_context(nc.psum_tensor("ff_ps_d", [P, TB, C], F32))

        consts_loaded, half_set, passed = sem("consts_loaded"), sem("half_set2"), sem("passed")
        blk_loaded, x1_turned, x1_hi_done, x1_lo_done = (
            sem("blk_loaded"), sem("x1_turned"), sem("x1_hi_done"), sem("x1_lo_done"))
        gate_ready, up_ready, gate_done, fuse_done, fuse_hi_done, fuse_lo_done, down_done = (
            sem("gate_ready"), sem("up_ready"), sem("gate_done"), sem("fuse_done"), sem("fuse_hi_done"),
            sem("fuse_lo_done"), sem("down_done"))
        z_scaled, z_done, stats_done, var_done, rstd_done, result_done, stored = (
            sem("z_scaled"), sem("z_done"), sem("stats_done2"), sem("var_done2"), sem("rstd_done2"),
            sem("result_done"), [sem(f"stored{t}") for t in range(TB)])
        B2 = 2

        w_gate = w_ffn_sb[:, 0:4, :]
        w_up = w_ffn_sb[:, 4:8, :]
        w_down = w_ffn_sb[:, 8:12, :].rearrange("p c (o n) -> p (c o) n", n=C)

        with nc.Block() as block:
            @block.sync
            def _(sp):
                for t in range(TB):
                    sp.sem_inc(stored[t], 16)
                sp.dma_start(s_gu[:], scales).then_inc(consts_loaded, 16)
                sp.dma_start(s_dn[:], s_down.unsqueeze(0).to_broadcast([P, C])).then_inc(consts_loaded, 16)
                with sp.Fori(0, NB) as b:
                    sp.wait_ge(x1_turned, b * KC + KC)
                    sp.dma_start(x1_blk, x1_all[:, bass.ds(b * TB, TB), :]).then_inc(blk_loaded, 16)
                    for t in range(TB):
                        sp.wait_ge(result_done, b * TB + (TB + t + 1))
                        sp.dma_start(out[b * TB + t], result[:, t, :]).then_inc(stored[t], 16)
                for t in range(TB):
                    sp.wait_ge(stored[t], 16 * (NB + 1))

            @block.gpsimd
            def _(pool):
                pool.sem_inc(fuse_lo_done, B2)
                nc.gpsimd.memset(half[:], -0.5).then_inc(half_set, 1)
                pool.wait_ge(half_set, 1)
                with pool.Fori(0, NB) as b:
                    for o in range(NO):
                        pool.wait_ge(fuse_hi_done, b * NO + (o + 1))
                        pool.wait_ge(down_done, b * NO + (o + 1))
                        nc.gpsimd.tensor_tensor(fuse_lo[:, o % 2, :], fuse[:, o % 2, :],
                                                fuse_hi[:, o % 2, :].bitcast(F32), ALU.subtract).then_inc(fuse_lo_done, 1)
                    pool.wait_ge(var_done, b + 1)
                    nc.gpsimd.tensor_tensor(rstd[:], var_eps[:], half[:], ALU.pow).then_inc(rstd_done, 1)

            @block.tensor
            def _(pe):
                pe.sem_inc(x1_turned, KC)
                pe.sem_inc(down_done, B2)
                with pe.Fori(0, NB) as b:
                    pe.wait_ge(blk_loaded, b * 16 + 16)
                    pe.wait_ge(z_scaled, b * TB + TB)
                    for k in range(KC):
                        for t in range(TB):
                            last = nc.tensor.transpose(ps_d[:, k, t * P:(t + 1) * P],
                                                       x1_blk[:, t, k * P:(k + 1) * P], ident[:])
                        last.then_inc(x1_turned, 1)

                    def down(o):
                        pe.wait_ge(fuse_hi_done, b * NO + (o + 1))
                        for n, f in enumerate((fuse_hi, fuse_lo)):
                            if n == 1:
                                pe.wait_ge(fuse_lo_done, b * NO + (B2 + o + 1))
                            for t in range(TB):
                                last = nc.tensor.matmul(ps_d[:, t, :], f[:, o % 2, t * P:(t + 1) * P], w_down[:, o, :],
                                                        start=(o == 0 and n == 0), stop=(o == NO - 1 and n == 1))
                        last.then_inc(down_done, 1)

                    for o in range(NO):
                        for ps, w, ready, free in ((ps_g, w_gate, gate_ready, gate_done), (ps_u, w_up, up_ready, fuse_done)):
                            pe.wait_ge(free, b * NO + (o + 1))
                            for n, m in enumerate((x1t_hi, x1t_lo)):
                                for k in range(KC):
                                    if o == 0 and ps is ps_g:
                                        pe.wait_ge((x1_hi_done, x1_lo_done)[n], b * KC + (k + 1))
                                    last = nc.tensor.matmul(ps[:, o % 2, :], w[:, k, o * P:(o + 1) * P], m[:, k, :],
                                                            start=(n == 0 and k == 0), stop=(n == 1 and k == KC - 1))
                            last.then_inc(ready, 1)
                        if o >= 1:
                            down(o - 1)
                    down(NO - 1)

            @block.scalar
            def _(act):
                act.sem_inc(gate_done, B2)
                act.wait_ge(consts_loaded, 32)
                with act.Fori(0, NB) as b:
                    for k in range(KC):
                        act.wait_ge(x1_turned, b * KC + (KC + k + 1))
                        nc.scalar.activation(x1t_hi[:, k, :], ps_d[:, k, :], ACT.Copy).then_inc(x1_hi_done, 1)

                    def fuse_high(o):
                        act.wait_ge(fuse_done, b * NO + (B2 + o + 1))
                        act.wait_ge(down_done, b * NO + (o + 1))
                        nc.scalar.activation(fuse_hi[:, o % 2, :], fuse[:, o % 2, :], ACT.Copy).then_inc(fuse_hi_done, 1)

                    for o in range(NO):
                        act.wait_ge(gate_ready, b * NO + (o + 1))
                        act.wait_ge(fuse_done, b * NO + (o + 1))
                        nc.scalar.activation(gate[:, o % 2, :], ps_g[:, o % 2, :], ACT.Silu,
                                             scale=s_gu[:, 0, o:o + 1]).then_inc(gate_done, 1)
                        fuse_high(o)

            @block.vector
            def _(dve):
                dve.sem_inc(z_scaled, TB)
                dve.sem_inc(fuse_done, B2)
                dve.sem_inc(result_done, TB)
                dve.wait_ge(consts_loaded, 32)
                with dve.Fori(0, NB) as b:
                    for k in range(KC):
                        dve.wait_ge(x1_hi_done, b * KC + (k + 1))
                        nc.vector.tensor_tensor(x1t_lo[:, k, :], ps_d[:, k, :], x1t_hi[:, k, :].bitcast(F32),
                                                ALU.subtract).then_inc(x1_lo_done, 1)
                    for o in range(NO):
                        dve.wait_ge(up_ready, b * NO + (o + 1))
                        dve.wait_ge(gate_done, b * NO + (B2 + o + 1))
                        dve.wait_ge(fuse_lo_done, b * NO + (o + 1))
                        nc.vector.scalar_tensor_tensor(fuse[:, o % 2, :], ps_u[:, o % 2, :], s_gu[:, 1, o:o + 1],
                                                       gate[:, o % 2, :], ALU.mult, ALU.mult).then_inc(fuse_done, 1)
                    dve.wait_ge(down_done, b * NO + (B2 + NO))
                    dve.wait_ge(result_done, b * TB + TB)
                    for t in range(TB):
                        nc.vector.tensor_tensor(z[:, t, :], ps_d[:, t, :], s_dn[:], ALU.mult).then_inc(z_scaled, 1)
                    for t in range(TB):
                        dve.wait_ge(z_scaled, b * TB + (TB + t + 1))
                        nc.vector.tensor_tensor(z[:, t, :], z[:, t, :], x1_all[:, b * TB + t, :], ALU.add).then_inc(z_done, 1)
                    for t in range(TB):
                        dve.wait_ge(z_done, b * TB + (t + 1))
                        nc.vector.bn_stats(stats[:, t, :], z[:, t, :]).then_inc(stats_done, 1)
                    dve.wait_ge(stats_done, b * (2 * TB) + TB)
                    dve.sem_inc(passed, 1)
                    for t in range(TB):
                        nc.vector.bn_aggr(mean_var[:, t, :], stats[:, t, :]).then_inc(stats_done, 1)
                    dve.wait_ge(stats_done, b * (2 * TB) + 2 * TB)
                    nc.vector.tensor_scalar(var_eps[:], mean_var[:, :, 1], LN_EPS, None, ALU.add).then_inc(var_done, 1)
                    dve.wait_ge(rstd_done, b + 1)
                    for t in range(TB):
                        dve.wait_ge(stored[t], b * 16 + 16)
                        nc.vector.tensor_scalar(result[:, t, :], z[:, t, :], mean_var[:, t, 0:1], rstd[:, t:t + 1],
                                                ALU.subtract, ALU.mult).then_inc(result_done, 1)


def build(nc, x, w_qkv, w_o, rope, w_ffn, scales, s_down, out):
    xt = x.rearrange("(t p) c -> t p c", p=P)
    with ExitStack() as ctx:
        def sb(name, shape, dt):
            return ctx.enter_context(nc.sbuf_tensor(name, shape, dt))

        ident = sb("ident", [P, P], F32)
        q_all = sb("q_all", [P, G, T], F32)
        k_all = sb("k_all", [P, G, T], F32)
        with nc.sbuf_tensor("v_all", [P, T // P, C], F32) as v_all:
            project_program(nc, x.rearrange("(b t p) c -> b p t c", p=P, t=TB), w_qkv, rope, q_all, k_all, v_all, ident)
            attention_program(nc, q_all, k_all, v_all, ident)
        x1_all = k_all[:].rearrange("p g (t c) -> p (g t) c", c=C)
        w_ffn_sb = sb("w_ffn_sb", [P, NCH, INTER], F32R)
        output_program(nc, xt, w_o, w_ffn, q_all, x1_all, w_ffn_sb, ident)
        ffn_program(nc, scales, s_down, out.rearrange("(t p) c -> t p c", p=P), x1_all, w_ffn_sb, ident, q_all)


def kernel(**inputs):
    import numpy as np
    import concourse.bacc as bacc
    from concourse.bass_utils import run_bass_kernel_spmd

    w = {n: np.asarray(inputs["L0_attn_w_" + n]) for n in "qkvo"}
    gate, up, down = (np.asarray(inputs["L0_ffn_w_" + n]) for n in ("gate", "up", "down"))
    inv_freq = np.float32(1) / np.power(np.float32(10000), np.arange(HD // 2, dtype=np.float32) / np.float32(HD // 2))
    angle = np.outer(inv_freq, np.arange(T, dtype=np.float32)).astype(np.float32)
    cos, sin = np.cos(angle), np.sin(angle)
    rope = np.stack([np.concatenate([cos, cos]), np.concatenate([-sin, sin])], axis=1)
    arrays = {
        "x": np.asarray(inputs["L0_attn_x"]).reshape(T, C),
        "w_qkv": np.concatenate([w["q"], w["k"], w["v"]]).reshape(3 * G, P, C),
        "w_o": w["o"].reshape(G, P, C),
        "rope": rope.reshape(HD, 2, NB, BLK).transpose(2, 0, 1, 3),
        "w_ffn": np.concatenate([gate.reshape(4, P, INTER), up.reshape(4, P, INTER),
                                 down.reshape(4, 4, P, C).transpose(0, 2, 1, 3).reshape(4, P, INTER)]),
        "scales": np.stack([np.asarray(inputs["L0_ffn_s_gate"]).reshape(NO, P),
                            np.asarray(inputs["L0_ffn_s_up"]).reshape(NO, P)]).transpose(2, 0, 1),
        "s_down": np.asarray(inputs["L0_ffn_s_down"]),
    }
    arrays = {n: np.ascontiguousarray(a) for n, a in arrays.items()}
    arrays["w_ffn"] = arrays["w_ffn"].view(np.int32)
    nc = bacc.Bacc("TRN2", target_bir_lowering=False, num_devices=1)
    args = {n: nc.dram_tensor(n, a.shape, mybir.dt.from_np(a.dtype), kind="ExternalInput").ap() for n, a in arrays.items()}
    out = nc.dram_tensor("out", (T, C), F32, kind="ExternalOutput").ap()
    build(nc, **args, out=out)
    r = run_bass_kernel_spmd(nc, [arrays], core_ids=[0])
    return r.results[0]["out"].reshape(1, T, C)
```

```python
from contextlib import ExitStack

import concourse.bass as bass
from concourse import mybir

ALU = mybir.AluOpType
ACT = mybir.ActivationFunctionType
AX_X = mybir.AxisListType.X
F32 = mybir.dt.float32
F32R = mybir.dt.float32r
BF16 = mybir.dt.bfloat16
I8 = mybir.dt.int8
I32 = mybir.dt.int32

P = 128
T = 2048
C = 512
INTER = 2048
HD = 32
KC = C // P
HG = P // HD
G = C // P
BLK = 512
NB = T // BLK
TB = BLK // P
QGRP = 128
SCALE = float(HD) ** -0.5
W_EPS = 1e-8
LN_EPS = 1e-5
LOWEST = -3.0e38
MROW = 3 * HD
NCH = 12
NO = INTER // P




QSTEPS = 4


def quantize_tile(dve, nc, raw, wide, small, step, base, k):
    nc.vector.tensor_reduce(small[:, 0:4], raw.rearrange("p (g c) -> p g c", c=QGRP), AX_X, ALU.add,
                            apply_absolute_value=True).then_inc(step, 1)
    dve.wait_ge(step, base + k + 1)
    nc.vector.tensor_scalar(small[:, 4:8], small[:, 0:4], 1.0 / QGRP, W_EPS, ALU.mult, ALU.max).then_inc(step, 1)
    dve.wait_ge(step, base + k + 2)
    nc.vector.tensor_scalar(small[:, 8:12], small[:, 4:8], 0.5, None, ALU.mult)
    nc.vector.tensor_scalar(small[:, 12:16], small[:, 4:8], -0.5, None, ALU.mult).then_inc(step, 1)
    dve.wait_ge(step, base + k + 3)
    for g in range(C // QGRP):
        cols = slice(g * QGRP, (g + 1) * QGRP)
        nc.vector.tensor_scalar(wide[:, 0, cols], raw[:, cols], small[:, 8 + g:9 + g], small[:, 4 + g:5 + g],
                                ALU.is_gt, ALU.mult)
        last = nc.vector.tensor_scalar(wide[:, 1, cols], raw[:, cols], small[:, 12 + g:13 + g],
                                       small[:, 4 + g:5 + g], ALU.is_lt, ALU.mult)
    last.then_inc(step, 1)
    dve.wait_ge(step, base + k + 4)



def project_program(nc, x, w_qkv, w_o, rope, parts, v_all, wo_hi, wo_lo, ident):
    NT = 3 * G
    NP = 2 * G + TB
    NR = 2 * G
    with ExitStack() as ctx:
        def sb(name, shape, dt):
            return ctx.enter_context(nc.sbuf_tensor("pj_" + name, shape, dt))

        def sem(name):
            return ctx.enter_context(nc.semaphore("pj_" + name))

        wt_hi = sb("wt_hi", [P, NT, KC, P], F32R)
        wt_lo = sb("wt_lo", [P, NT, KC, P], F32R)
        w_raw = sb("w_raw", [P, 2, C], F32)
        w_q = sb("w_q", [P, 2, 2, C], F32)
        w_small = sb("w_small", [P, 2, 16], F32)
        x_nat = sb("x_nat", [P, TB, C], F32)
        xt_hi = sb("xt_hi", [P, KC, BLK], F32R)
        xt_lo = sb("xt_lo", [P, KC, BLK], F32R)
        rope_t = sb("rope_t", [P, 2, BLK], F32)
        proj = sb("proj", [P, 2, BLK], F32)
        turned = sb("turned", [P, 2, BLK], F32)
        by_cos = sb("by_cos", [P, 2, BLK], F32)
        rotated = sb("rotated", [P, 2, BLK], F32)
        split = sb("split", [P, 4, 2, BLK], F32R)
        ps_t = ctx.enter_context(nc.psum_tensor("pj_ps_t", [P, KC, BLK], F32))
        ps_o = ctx.enter_context(nc.psum_tensor("pj_ps_o", [P, 4, BLK], F32))

        ident_zero, ident_ready, passed = sem("ident_zero"), sem("ident_ready"), sem("passed")
        w_loaded = [sem("w_loaded0"), sem("w_loaded1")]
        w_step, w_signs, w_sub, w_ste = sem("w_step"), sem("w_signs"), sem("w_sub"), sem("w_ste")
        w_turned, w_hi_done, w_lo_done = sem("w_turned"), sem("w_hi_done"), sem("w_lo_done")
        wo_loaded, wo_step, wo_signs, wo_sub, wo_ste = (
            sem("wo_loaded"), sem("wo_step"), sem("wo_signs"), sem("wo_sub"), sem("wo_ste"))
        wo_turned, wo_hi_done, wo_lo_done = sem("wo_turned"), sem("wo_hi_done"), sem("wo_lo_done")
        x_loaded, rope_loaded = sem("x_loaded"), sem("rope_loaded")
        x_turned, x_hi_done, x_lo_done = sem("x_turned"), sem("x_hi_done"), sem("x_lo_done")
        prod_ready, prod_copied = sem("prod_ready"), sem("prod_copied")
        turn_done, cos_done, sin_done, rope_done = sem("turn_done"), sem("cos_done"), sem("sin_done"), sem("rope_done")
        split_hi, split_lo, stored = sem("split_hi"), sem("split_lo"), [sem(f"stored{i}") for i in range(4)]
        W2, KC4, O4, R2, O1 = 2, KC, 4, 2, 1
        WO_AT = 5

        with nc.Block() as block:
            @block.sync
            def _(sp):
                with sp.Fori(0, NT // 2) as i:
                    for j in range(2):
                        sp.wait_ge(w_ste, i * 2 + (j + 1))
                        sp.dma_start(w_raw[:, j, :], w_qkv[i * 2 + j]).then_inc(w_loaded[j], 16)
                for s in stored:
                    sp.sem_inc(s, 16)
                sp.wait_ge(w_ste, NT + W2)
                with sp.Fori(0, NB) as b:
                    sp.wait_ge(x_turned, b * KC + KC4)
                    sp.dma_start(x_nat[:], x[b]).then_inc(x_loaded, 16)
                    sp.wait_ge(wo_ste, b + O1)
                    sp.dma_start(w_raw[:, 0, :], w_o[b]).then_inc(wo_loaded, 16)
                    sp.wait_ge(rope_done, b * NR + R2)
                    sp.dma_start(rope_t[:], rope[b]).then_inc(rope_loaded, 16)
                    for i in range(NR):
                        sp.wait_ge(split_lo, b * NR + (O4 + i + 1))
                        sp.dma_start(parts[i // G, i % G, b], split[:, i % 4, :, :].bitcast(F32)).then_inc(stored[i % 4], 16)
                for s in stored:
                    sp.wait_ge(s, 16 * (NB * NR // 4 + 1))

            @block.gpsimd
            def _(pool):
                def straight_through(j, signs, sub, n, ste):
                    pool.wait_ge(signs, n)
                    nc.gpsimd.tensor_tensor(w_q[:, j, 1, :], w_q[:, j, 0, :], w_raw[:, j, :],
                                            ALU.subtract).then_inc(sub, 1)
                    pool.wait_ge(sub, n)
                    nc.gpsimd.tensor_tensor(w_q[:, j, 0, :], w_raw[:, j, :], w_q[:, j, 1, :],
                                            ALU.add).then_inc(ste, 1)

                pool.sem_inc(w_ste, W2)
                pool.sem_inc(wo_ste, O1)
                pool.sem_inc(split_lo, O4)
                nc.gpsimd.memset(ident[:], 0.0).then_inc(ident_zero, 1)
                pool.wait_ge(ident_zero, 1)
                nc.gpsimd.affine_select(out=ident[:], in_=ident[:], compare_op=ALU.not_equal, fill=1.0, base=0,
                                        pattern=[[-1, P]], channel_multiplier=1).then_inc(ident_ready, 1)
                with pool.Fori(0, NT // 2) as i:
                    for j in range(2):
                        straight_through(j, w_signs, w_sub, i * 2 + (j + 1), w_ste)
                with pool.Fori(0, NB) as b:
                    straight_through(0, wo_signs, wo_sub, b + 1, wo_ste)
                    pool.wait_ge(rope_loaded, b * 16 + 16)

                    def low(i):
                        pool.wait_ge(split_hi, b * NR + (i + 1))
                        nc.gpsimd.tensor_tensor(split[:, i % 4, 1, :], rotated[:, i % 2, :],
                                                split[:, i % 4, 0, :].bitcast(F32), ALU.subtract).then_inc(split_lo, 1)

                    for i in range(NR):
                        pool.wait_ge(prod_copied, b * NP + (O4 + i + 1))
                        pool.wait_ge(rope_done, b * NR + (i + 1))
                        nc.gpsimd.tensor_tensor(by_cos[:, i % 2, :], proj[:, i % 2, :], rope_t[:, 0, :],
                                                ALU.mult).then_inc(cos_done, 1)
                        if i:
                            low(i - 1)
                    low(NR - 1)

            @block.tensor
            def _(pe):
                pe.sem_inc(w_turned, W2)
                pe.sem_inc(x_turned, KC4)
                pe.wait_ge(ident_ready, 1)
                with pe.Fori(0, NT // 2) as i:
                    for j in range(2):
                        pe.wait_ge(w_ste, i * 2 + (W2 + j + 1))
                        pe.wait_ge(w_lo_done, i * 2 + (j + 1))
                        for k in range(KC):
                            last = nc.tensor.transpose(ps_t[:, j, k * P:(k + 1) * P],
                                                       w_q[:, j, 0, k * P:(k + 1) * P], ident[:])
                        last.then_inc(w_turned, 1)
                pe.wait_ge(w_lo_done, NT + W2)
                with pe.Fori(0, NB) as b:
                    pe.wait_ge(x_loaded, b * 16 + 16)
                    pe.wait_ge(wo_lo_done, b + O1)
                    for k in range(KC):
                        pe.wait_ge(x_lo_done, b * KC + (k + 1))
                        for t in range(TB):
                            last = nc.tensor.transpose(ps_t[:, k, t * P:(t + 1) * P],
                                                       x_nat[:, t, k * P:(k + 1) * P], ident[:])
                        last.then_inc(x_turned, 1)
                    for i in range(NP):
                        pe.wait_ge(prod_copied, b * NP + (i + 1))
                        if i < NR:
                            terms = [(wt_hi, xt_hi), (wt_hi, xt_lo), (wt_lo, xt_hi)]
                        else:
                            terms = [(xt_hi, wt_hi), (xt_lo, wt_hi), (xt_hi, wt_lo)]
                        for n, (w, m) in enumerate(terms):
                            for k in range(KC):
                                if i == 0 and n < 2:
                                    part_done = (x_hi_done, x_lo_done)[n]
                                    pe.wait_ge(part_done, b * KC + ((KC4 if n == 1 else 0) + k + 1))
                                if i < NR:
                                    lhs, rhs = w[:, i, k, :], m[:, k, :]
                                else:
                                    lhs, rhs = w[:, k, (i - NR) * P:(i - NR + 1) * P], m[:, 2 * G:3 * G, k, :]
                                last = nc.tensor.matmul(ps_o[:, i % 4, :], lhs, rhs,
                                                        start=(n == 0 and k == 0), stop=(n == 2 and k == KC - 1))
                        last.then_inc(prod_ready, 1)
                        if i == WO_AT:
                            pe.wait_ge(wo_ste, b + (O1 + 1))
                            for k in range(KC):
                                last = nc.tensor.transpose(ps_t[:, 0, k * P:(k + 1) * P],
                                                           w_q[:, 0, 0, k * P:(k + 1) * P], ident[:])
                            last.then_inc(wo_turned, 1)

            @block.scalar
            def _(act):
                act.sem_inc(prod_copied, O4)
                with act.Fori(0, NT // 2) as i:
                    for j in range(2):
                        act.wait_ge(w_turned, i * 2 + (W2 + j + 1))
                        nc.scalar.activation(wt_hi[:, i * 2 + j, :, :],
                                             ps_t[:, j, :].rearrange("p (k c) -> p k c", c=P),
                                             ACT.Copy).then_inc(w_hi_done, 1)
                with act.Fori(0, NB) as b:
                    for k in range(KC):
                        act.wait_ge(x_turned, b * KC + (KC4 + k + 1))
                        nc.scalar.activation(xt_hi[:, k, :], ps_t[:, k, :], ACT.Copy).then_inc(x_hi_done, 1)
                    def high(i):
                        act.wait_ge(rope_done, b * NR + (R2 + i + 1))
                        act.wait_ge(stored[i % 4], b * (16 * NR // 4) + 16 * (i // 4 + 1))
                        nc.scalar.activation(split[:, i % 4, 0, :], rotated[:, i % 2, :], ACT.Copy).then_inc(split_hi, 1)

                    for i in range(NP):
                        act.wait_ge(prod_ready, b * NP + (i + 1))
                        if i < NR:
                            act.wait_ge(rope_done, b * NR + (i + 1))
                            nc.scalar.activation(proj[:, i % 2, :], ps_o[:, i % 4, :],
                                                 ACT.Copy).then_inc(prod_copied, 1)
                        else:
                            nc.scalar.activation(v_all[:, b * TB + (i - NR), :], ps_o[:, i % 4, :],
                                                 ACT.Copy).then_inc(prod_copied, 1)
                        if 1 <= i <= NR:
                            high(i - 1)
                        if i == WO_AT + 1:
                            act.wait_ge(wo_turned, b + 1)
                            nc.scalar.activation(wo_hi[:, b, :, :], ps_t[:, 0, :].rearrange("p (k c) -> p k c", c=P),
                                                 ACT.Copy).then_inc(wo_hi_done, 1)

            @block.vector
            def _(dve):
                dve.sem_inc(w_lo_done, W2)
                dve.sem_inc(wo_lo_done, O1)
                dve.sem_inc(x_lo_done, KC4)
                dve.sem_inc(rope_done, R2)
                STEPS = 2 * QSTEPS
                with dve.Fori(0, NT // 2) as i:
                    for j in range(2):
                        dve.wait_ge(w_loaded[j], i * 16 + 16)
                        dve.wait_ge(w_turned, i * 2 + (j + 1))
                        quantize_tile(dve, nc, w_raw[:, j, :], w_q[:, j], w_small[:, j], w_step, i * STEPS, j * QSTEPS)
                        nc.vector.tensor_tensor(w_q[:, j, 0, :], w_q[:, j, 0, :], w_q[:, j, 1, :],
                                                ALU.subtract).then_inc(w_signs, 1)
                    for j in range(2):
                        dve.wait_ge(w_hi_done, i * 2 + (j + 1))
                        nc.vector.tensor_tensor(wt_lo[:, i * 2 + j, :, :],
                                                ps_t[:, j, :].rearrange("p (k c) -> p k c", c=P),
                                                wt_hi[:, i * 2 + j, :, :].bitcast(F32), ALU.subtract).then_inc(w_lo_done, 1)
                dve.wait_ge(w_turned, NT + W2)
                swap = [(r + HD // 2) % HD for r in range(HD)]
                with dve.Fori(0, NB) as b:
                    for k in range(KC):
                        dve.wait_ge(x_hi_done, b * KC + (k + 1))
                        nc.vector.tensor_tensor(xt_lo[:, k, :], ps_t[:, k, :], xt_hi[:, k, :].bitcast(F32),
                                                ALU.subtract).then_inc(x_lo_done, 1)
                    dve.wait_ge(wo_loaded, b * 16 + 16)
                    quantize_tile(dve, nc, w_raw[:, 0, :], w_q[:, 0], w_small[:, 0], wo_step, b * QSTEPS, 0)
                    nc.vector.tensor_tensor(w_q[:, 0, 0, :], w_q[:, 0, 0, :], w_q[:, 0, 1, :],
                                            ALU.subtract).then_inc(wo_signs, 1)
                    dve.wait_ge(rope_loaded, b * 16 + 16)
                    for i in range(NR):
                        dve.wait_ge(prod_copied, b * NP + (O4 + i + 1))
                        dve.sem_inc(passed, 1)
                        nc.vector.stream_shuffle(turned[:, i % 2, :], proj[:, i % 2, :], swap).then_inc(turn_done, 1)
                        dve.wait_ge(turn_done, b * NR + (i + 1))
                        nc.vector.tensor_tensor(turned[:, i % 2, :], turned[:, i % 2, :], rope_t[:, 1, :],
                                                ALU.mult).then_inc(sin_done, 1)
                        dve.wait_ge(sin_done, b * NR + (i + 1))
                        dve.wait_ge(cos_done, b * NR + (i + 1))
                        if i >= 2:
                            dve.wait_ge(split_lo, b * NR + (O4 + i - 1))
                        nc.vector.tensor_tensor(rotated[:, i % 2, :], by_cos[:, i % 2, :], turned[:, i % 2, :],
                                                ALU.add).then_inc(rope_done, 1)
                        if i == WO_AT + 2:
                            dve.wait_ge(wo_hi_done, b + 1)
                            nc.vector.tensor_tensor(wo_lo[:, b, :, :], ps_t[:, 0, :].rearrange("p (k c) -> p k c", c=P),
                                                    wo_hi[:, b, :, :].bitcast(F32), ALU.subtract).then_inc(wo_lo_done, 1)


AU = [16 * (b + 1) for b in range(NB)]
KT = [TB * (b + 1) for b in range(NB)]
NA, NK = sum(AU), sum(KT)
CUM_K = [sum(KT[:b]) for b in range(NB + 1)]
SPREAD = [(2, 1.3, 10.8), (3, 11.2, 22.8), (0, 30.5, 34.0), (1, 34.5, 39.4)]
ORDINAL = {m: n for n, (m, _, _) in enumerate(SPREAD)}


def units(b):
    return [(j, qt, c) for c in range(b + 1) for qt in range(TB) for j in range(HG)]


def block_of(t):
    b = max(b for b in range(NB) if CUM_K[b] <= t)
    return b, t - CUM_K[b]


def first_query(t):
    b, i = block_of(t)
    return max(0, i - (KT[b] - TB)) * P


def pass_order(last):
    base, marks = [], []
    for t in range(NK + 1):
        if t < NK:
            width = 1 - first_query(t) / BLK
            base += [(("scores", t, 0), t, 0.4 * width), (("scores", t, 1), t, 0.4 * width)]
        if t:
            b, i = block_of(t - 1)
            width = 1 - first_query(t - 1) / BLK
            base += [(("sums", t - 1), t, width), (("values", t - 1), t, width)]
            if i == KT[b] - 1:
                base.append((("copy", b), t, 0))
    between = []
    for m, start, end in SPREAD:
        if last and m < 2:
            continue
        for u in range(AU[m]):
            between.append((start + (end - start) * u / (AU[m] - 1), ("max", m, u)))
        between += [(end + 0.01, ("finish", m)), (end + 0.45, ("turn", m))]
    for b in range(NB):
        for k in range(TB):
            between.append((CUM_K[b + 1] + 0.8 + 0.35 * k, ("invert", b, k)))
        between.append((CUM_K[b + 1] + 2.3, ("scale", b)))
    between.sort(key=lambda e: e[0])
    order, spent, total = [], {}, {}
    for _, t, w in base:
        total[t] = total.get(t, 0) + w
    for step, t, w in base:
        at = t + spent.get(t, 0) / total[t]
        while between and between[0][0] <= at:
            order.append(between.pop(0)[1])
        order.append(step)
        spent[t] = spent.get(t, 0) + w
    return order + [step for _, step in between]


def attention_program(nc, parts, y_all, v_all, ident):
    with ExitStack() as ctx:
        def sb(name, shape, dt):
            return ctx.enter_context(nc.sbuf_tensor("at_" + name, shape, dt))

        def sem(name):
            return ctx.enter_context(nc.semaphore("at_" + name))

        k_stack = sb("k_stack", [P, HG, T], F32R)
        q_stack = sb("q_stack", [P, NB, HG, BLK], F32R)
        v_grp = sb("v_grp", [P, T // P, P], F32)
        probs = sb("probs", [P, 2, HG, BLK], F32)
        tail = sb("tail", [P, HG], F32)
        strip = sb("strip", [P, BLK], F32)
        spill = sb("spill", [P, 2, BLK], BF16)
        ones = sb("ones", [P, HD], F32)
        part_max = sb("part_max", [P, 2, TB * HG, NB], F32)
        neg_max = sb("neg_max", [P, 2, TB * HG], F32)
        neg_max_hi = sb("neg_max_hi", [P, 2, TB * HG], F32R)
        turn_in = sb("turn_in", [P, 2, TB, P], F32)
        row_sums = sb("row_sums", [P, 2, BLK], F32)
        y_raw = sb("y_raw", [P, 2, BLK], F32)
        ps_m = ctx.enter_context(nc.psum_tensor("at_ps_m", [P, 2, BLK], F32))
        ps_s = ctx.enter_context(nc.psum_tensor("at_ps_s", [P, HG, BLK], F32))
        ps_y = ctx.enter_context(nc.psum_tensor("at_ps_y", [P, BLK], F32))
        ps_l = ctx.enter_context(nc.psum_tensor("at_ps_l", [P, BLK], F32))

        const_step, consts_ready, ones_rows = sem("const_step"), sem("consts_ready"), sem("ones_rows")
        q_loaded = [sem(f"q_loaded{b}") for b in range(NB)]
        k_loaded = [sem(f"k_loaded{b}") for b in range(NB)]
        v_loaded = [sem(f"v_loaded{b}") for b in range(NB)]
        unit_ready, unit_drained = sem("unit_ready"), sem("unit_drained")
        max_step, max_ready, max_turned, max_placed = (
            sem("max_step"), sem("max_ready"), sem("max_turned"), sem("max_placed"))
        scores_ready, exp_done, masked, values_done = (
            sem("scores_ready"), sem("exp_done"), sem("masked"), sem("values_done"))
        sums_copied, inverted, scaled, passed = sem("sums_copied"), sem("inverted"), sem("scaled"), sem("passed")
        V2, C1 = 2, 1
        LOADS = 16 * 3
        U0 = AU[0] + AU[1]
        PH = 2

        def passes(eng, body):
            with eng.Fori(0, G - 1) as g:
                body(g, False)
            body(G - 1, True)

        def before(m):
            return PH + ORDINAL[m]

        with nc.Block() as block:
            @block.gpsimd
            def _(pool):
                nc.gpsimd.memset(tail[:], 0.0).then_inc(const_step, 1)
                nc.gpsimd.memset(strip[:], 0.0).then_inc(const_step, 1)
                pool.wait_ge(const_step, 2)
                for r in range(2):
                    nc.gpsimd.affine_select(out=tail[:], in_=tail[:], compare_op=ALU.not_equal, fill=1.0,
                                            base=-MROW - r, pattern=[[-2, HG]], channel_multiplier=1).then_inc(const_step, 1)
                    pool.wait_ge(const_step, 3 + r)
                nc.gpsimd.memset(turn_in[:], 0.0).then_inc(consts_ready, 1)
                nc.gpsimd.memset(ones[:], 1.0).then_inc(consts_ready, 1)
                nc.gpsimd.affine_select(out=strip[:], in_=strip[:], compare_op=ALU.is_ge, fill=LOWEST, base=BLK - P,
                                        pattern=[[-1, BLK]], channel_multiplier=1).then_inc(consts_ready, 1)

                def body(g, last):
                    for step in pass_order(last):
                        if step[0] == "scores":
                            _, t, pair = step
                            b, i = block_of(t)
                            if i < KT[b] - TB:
                                continue
                            pool.wait_ge(exp_done, g * (2 * NK) + (2 * t + pair + 1))
                            pool.sem_inc(passed, 1)
                            lo = first_query(t)
                            tri = probs[:, t % 2, 2 * pair:2 * pair + 2, lo:lo + P]
                            nc.gpsimd.affine_select(out=tri, in_=tri, compare_op=ALU.is_ge, fill=0.0, base=0,
                                                    pattern=[[0, 2], [1, P]], channel_multiplier=-1).then_inc(masked, 1)
                passes(pool, body)

            @block.sync
            def _(sp):
                def load(stack, b, w, g, order, done):
                    for r, part in enumerate(order):
                        src = parts[w, g, b].rearrange("(j d) r t -> d j r t", d=HD)[:, :, part, :]
                        sp.dma_start(stack[r * HD:(r + 1) * HD].bitcast(F32), src).then_inc(done, 16)

                def load_q(g, b):
                    load(q_stack[:, b, :, :], b, 0, g, (0, 0, 1), q_loaded[b])

                def load_k(g, b):
                    load(k_stack[:, :, b * BLK:(b + 1) * BLK], b, 1, g, (0, 1, 0), k_loaded[b])

                def load_v(g, b):
                    sp.dma_start(v_grp[:, b * TB:(b + 1) * TB, :],
                                 v_all[:, b * TB:(b + 1) * TB, bass.ds(g * P, P)]).then_inc(v_loaded[b], 16)

                for b in range(NB):
                    load_q(0, b)
                    load_k(0, b)
                    load_v(0, b)
                with sp.Fori(0, G - 1) as g:
                    for b in range(NB - 1):
                        sp.wait_ge(values_done, g * NK + (V2 + CUM_K[b + 1]))
                        load_q(g + 1, b)
                    for b in range(NB):
                        sp.wait_ge(values_done, g * NK + (V2 + CUM_K[NB - 1] + (b + 1) * TB))
                        load_k(g + 1, b)
                        load_v(g + 1, b)
                    load_q(g + 1, NB - 1)

            @block.tensor
            def _(pe):
                pe.sem_inc(values_done, V2)
                pe.wait_ge(consts_ready, 3)
                ring = []

                def wait_bank(g):
                    if len(ring) >= 2:
                        s, per, v = ring[-2]
                        pe.wait_ge(s, g * per + v)

                def unit(g, gq, m, u, drained):
                    j, qt, c = units(m)[u]
                    if u == 0:
                        pe.wait_ge(q_loaded[m], gq * LOADS + LOADS)
                    if u % (TB * HG) == 0:
                        pe.wait_ge(k_loaded[c], gq * LOADS + LOADS)
                    wait_bank(g)
                    w = BLK if c < m else (qt + 1) * P
                    nc.tensor.matmul(ps_m[:, len(ring) % 2, 0:w],
                                     q_stack[0:MROW, m, j, qt * P:(qt + 1) * P],
                                     k_stack[0:MROW, j, c * BLK:c * BLK + w], start=True, stop=True).then_inc(unit_ready, 1)
                    ring.append((unit_drained, NA, drained))

                def turn_maxima(g, m, n):
                    wait_bank(g)
                    pe.wait_ge(max_ready, g * NB + n)
                    for qt in range(TB):
                        last = nc.tensor.transpose(ps_m[:, len(ring) % 2, qt * P:(qt + 1) * P],
                                                   turn_in[:, m % 2, qt, :], ident[:])
                    last.then_inc(max_turned, 1)
                    ring.append((max_placed, NB, n))

                for m in range(PH):
                    for u in range(AU[m]):
                        unit(0, 0, m, u, (m * AU[0]) + u + 1)
                    turn_maxima(0, m, m + 1)
                pe.wait_ge(ones_rows, 2)

                def body(g, last):
                    del ring[:]
                    ring.extend([(unit_drained, NA, U0), (max_placed, NB, PH)])
                    drained = U0
                    for step in pass_order(last):
                        kind = step[0]
                        if kind == "scores":
                            _, t, pair = step
                            b, i = block_of(t)
                            if i == 0 and pair == 0:
                                pe.wait_ge(max_placed, g * NB + (b + 1))
                            if t >= 1:
                                pe.wait_ge(exp_done, g * (2 * NK) + (2 * (t - 1) + pair + 1))
                            lo = first_query(t)
                            for j in (2 * pair, 2 * pair + 1):
                                last_mm = nc.tensor.matmul(ps_s[:, j, lo:BLK], k_stack[:, j, i * P:(i + 1) * P],
                                                           q_stack[:, b, j, lo:BLK], start=True, stop=True)
                            last_mm.then_inc(scores_ready, 1)
                        elif kind in ("sums", "values"):
                            t = step[1]
                            b, i = block_of(t)
                            if kind == "sums":
                                if i == 0:
                                    pe.wait_ge(sums_copied, g * NB + (C1 + b))
                                if i >= KT[b] - TB:
                                    pe.wait_ge(masked, g * (2 * TB * NB) + 2 * (TB * b + i - (KT[b] - TB) + 1))
                                else:
                                    pe.wait_ge(exp_done, g * (2 * NK) + 2 * (t + 1))
                            elif b == NB - 1 and i % TB == 0 or i == 0:
                                pe.wait_ge(v_loaded[i // TB], g * 16 + 16)
                            lo = first_query(t)
                            for j in range(HG):
                                rows = slice(j * HD, (j + 1) * HD)
                                to, lhs = (ps_l, ones[:, :]) if kind == "sums" else (ps_y, v_grp[:, i, rows])
                                last_mm = nc.tensor.matmul(to[rows, lo:BLK], lhs, probs[:, t % 2, j, lo:BLK],
                                                           start=(i == 0), stop=(i == KT[b] - 1))
                            if kind == "values":
                                last_mm.then_inc(values_done, 1)
                        elif kind == "max":
                            _, m, u = step
                            drained += 1
                            unit(g, g if m >= 2 else g + 1, m, u, drained)
                        elif kind == "turn":
                            turn_maxima(g, step[1], before(step[1]) + 1)
                passes(pe, body)

            @block.scalar
            def _(act):
                def place_maxima(g, m, n, r):
                    act.wait_ge(max_turned, g * NB + n)
                    nc.scalar.activation(q_stack[MROW:P, m, :, :],
                                         ps_m[MROW:P, r % 2, :].unsqueeze(1).to_broadcast([P - MROW, HG, BLK]),
                                         ACT.Copy).then_inc(max_placed, 1)

                act.sem_inc(sums_copied, C1)
                act.wait_ge(const_step, 4)
                nc.scalar.activation(k_stack[MROW:P, 2:4, :], tail[MROW:P, 2:4].unsqueeze(2).to_broadcast([P - MROW, 2, T]),
                                     ACT.Copy).then_inc(ones_rows, 1)
                place_maxima(0, 0, 1, AU[0])
                place_maxima(0, 1, 2, AU[0] + 1 + AU[1])

                def body(g, last):
                    r = 0
                    for step in pass_order(last):
                        if step[0] == "scores":
                            _, t, pair = step
                            lo = first_query(t)
                            act.wait_ge(scores_ready, g * (2 * NK) + (2 * t + pair + 1))
                            act.wait_ge(values_done, g * NK + (t + 1))
                            nc.scalar.activation(probs[:, t % 2, 2 * pair:2 * pair + 2, lo:BLK],
                                                 ps_s[:, 2 * pair:2 * pair + 2, lo:BLK], ACT.Exp,
                                                 scale=SCALE).then_inc(exp_done, 1)
                        elif step[0] == "copy":
                            b = step[1]
                            act.wait_ge(values_done, g * NK + (V2 + CUM_K[b + 1]))
                            act.wait_ge(scaled, g * NB + (b + 1))
                            nc.scalar.activation(row_sums[:, b % 2, :], ps_l[:], ACT.Copy)
                            nc.scalar.activation(y_raw[:, b % 2, :], ps_y[:], ACT.Copy).then_inc(sums_copied, 1)
                        elif step[0] == "max":
                            r += 1
                        elif step[0] == "turn":
                            place_maxima(g, step[1], before(step[1]) + 1, r)
                            r += 1
                passes(act, body)

            @block.vector
            def _(dve):
                dve.sem_inc(scaled, 2)
                dve.wait_ge(const_step, 4)
                nc.vector.tensor_copy(k_stack[MROW:P, 0:2, :],
                                      tail[MROW:P, 0:2].unsqueeze(2).to_broadcast([P - MROW, 2, T])).then_inc(ones_rows, 1)
                dve.wait_ge(consts_ready, 3)

                def drain_unit(g, m, u, r, drained, spilled):
                    j, qt, c = units(m)[u]
                    dve.wait_ge(unit_ready, g * NA + drained)
                    out = part_max[:, m % 2, qt * HG + j, c:c + 1]
                    if c < m:
                        nc.vector.tensor_reduce(out, ps_m[:, r % 2, :], AX_X, ALU.max).then_inc(unit_drained, 1)
                    else:
                        w = (qt + 1) * P
                        if len(spilled) >= 2:
                            dve.wait_ge(unit_drained, g * NA + spilled[-2])
                        dve.sem_inc(passed, 1)
                        nc.vector.tensor_tensor_reduce(spill[:, len(spilled) % 2, 0:w], ps_m[:, r % 2, 0:w],
                                                       strip[:, BLK - w:BLK], 1.0, LOWEST, ALU.add, ALU.max,
                                                       out).then_inc(unit_drained, 1)
                        spilled.append(drained)

                def finish_maxima(g, m, n, drained):
                    buf = m % 2
                    dve.wait_ge(unit_drained, g * NA + drained)
                    nc.vector.tensor_reduce(neg_max[:, buf, :], part_max[:, buf, :, 0:m + 1], AX_X, ALU.max,
                                            negate=True).then_inc(max_step, 1)
                    dve.wait_ge(max_step, g * (2 * NB) + (2 * n - 1))
                    nc.vector.tensor_copy(neg_max_hi[:, buf, :], neg_max[:, buf, :]).then_inc(max_step, 1)
                    dve.wait_ge(max_step, g * (2 * NB) + 2 * n)
                    to = turn_in[:, buf, :, MROW:MROW + 2 * HG].rearrange("p t (j r) -> p t j r", r=2)
                    hi = neg_max_hi[:, buf, :].bitcast(F32).rearrange("p (t j) -> p t j", j=HG)
                    nc.vector.tensor_copy(to[:, :, :, 0], hi)
                    nc.vector.tensor_tensor(to[:, :, :, 1], neg_max[:, buf, :].rearrange("p (t j) -> p t j", j=HG), hi,
                                            ALU.subtract).then_inc(max_ready, 1)

                spilled, drained = [], 0
                for m in range(PH):
                    for u in range(AU[m]):
                        drained += 1
                        drain_unit(0, m, u, drained - 1 + m, drained, spilled)
                    finish_maxima(0, m, m + 1, drained)

                def body(g, last):
                    r, drained, spilled = 0, U0, []
                    for step in pass_order(last):
                        kind = step[0]
                        if kind == "max":
                            drained += 1
                            drain_unit(g, step[1], step[2], r, drained, spilled)
                            r += 1
                        elif kind == "finish":
                            finish_maxima(g, step[1], before(step[1]) + 1, drained)
                        elif kind == "turn":
                            r += 1
                        elif kind == "invert":
                            _, b, k = step
                            cols = slice(k * P, (k + 1) * P)
                            if k == 0:
                                dve.wait_ge(sums_copied, g * NB + (C1 + b + 1))
                            nc.vector.reciprocal(row_sums[:, b % 2, cols], row_sums[:, b % 2, cols]).then_inc(inverted, 1)
                        elif kind == "scale":
                            b = step[1]
                            dve.wait_ge(inverted, g * (NB * TB) + (b + 1) * TB)
                            nc.vector.tensor_tensor(y_all[:, g, b * BLK:(b + 1) * BLK], y_raw[:, b % 2, :],
                                                    row_sums[:, b % 2, :], ALU.mult).then_inc(scaled, 1)
                passes(dve, body)


def output_program(nc, x, wo_hi, wo_lo, w_ffn, y_all, x1_all, w_ffn_sb):
    TT = T // P
    with ExitStack() as ctx:
        def sb(name, shape, dt):
            return ctx.enter_context(nc.sbuf_tensor("op_" + name, shape, dt))

        def sem(name):
            return ctx.enter_context(nc.semaphore("op_" + name))

        w_i8 = sb("w_i8", [P, 2, INTER // 4], I32)
        y_hi = sb("y_hi", [P, 2, KC, P], F32R)
        y_lo = sb("y_lo", [P, 2, KC, P], F32R)
        x_in = sb("x_in", [P, 2, C], F32)
        res = sb("res", [P, 2, C], F32)
        stats = sb("stats", [P, 2, 6], F32)
        mean_var = sb("mean_var", [P, 2, 2], F32)
        var_eps = sb("var_eps", [P, 2], F32)
        rstd = sb("rstd", [P, 2], F32)
        half = sb("half", [P, 1], F32)
        ps_o = ctx.enter_context(nc.psum_tensor("op_ps_o", [P, 2, C], F32))

        ffn_loaded, ffn_done = [sem("ffn_loaded0"), sem("ffn_loaded1")], sem("ffn_done")
        x_loaded = [sem("xin_loaded0"), sem("xin_loaded1")]
        half_set, passed = sem("half_set"), sem("passed")
        y_hi_done, y_lo_done, out_ready = sem("y_hi_done"), sem("y_lo_done"), sem("out_ready")
        res_done, stats_done, var_done, rstd_done, x1_done = (
            sem("res_done"), sem("stats_done"), sem("var_done"), sem("rstd_done"), sem("x1_done"))
        B2 = 2

        with nc.Block() as block:
            @block.sync
            def _(sp):
                with sp.Fori(0, NCH // 2) as i:
                    for j in range(2):
                        sp.wait_ge(res_done, i * 2 + (j + 1))
                        sp.dma_start(x_in[:, j, :], x[i * 2 + j]).then_inc(x_loaded[j], 16)
                        sp.wait_ge(ffn_done, i * 2 + (j + 1))
                        sp.dma_start(w_i8[:, j, :], w_ffn[i * 2 + j]).then_inc(ffn_loaded[j], 16)
                with sp.Fori(NCH // 2, TT // 2) as i:
                    for j in range(2):
                        sp.wait_ge(res_done, i * 2 + (j + 1))
                        sp.dma_start(x_in[:, j, :], x[i * 2 + j]).then_inc(x_loaded[j], 16)

            @block.gpsimd
            def _(pool):
                nc.gpsimd.memset(half[:], -0.5).then_inc(half_set, 1)
                pool.wait_ge(half_set, 1)
                with pool.Fori(0, TT // 2) as i:
                    for j in range(2):
                        pool.wait_ge(var_done, i * 2 + (j + 1))
                        nc.gpsimd.tensor_tensor(rstd[:, j:j + 1], var_eps[:, j:j + 1], half[:], ALU.pow).then_inc(rstd_done, 1)

            @block.tensor
            def _(pe):
                pe.sem_inc(out_ready, B2)
                with pe.Fori(0, TT // 2) as i:
                    for j in range(2):
                        pe.wait_ge(res_done, i * 2 + (j + 1))
                        pe.wait_ge(y_hi_done, i * 2 + (j + 1))
                        for n, (y, w) in enumerate(((y_hi, wo_hi), (y_hi, wo_lo), (y_lo, wo_hi))):
                            if n == 2:
                                pe.wait_ge(y_lo_done, i * 2 + (j + 1))
                            for k in range(KC):
                                last = nc.tensor.matmul(ps_o[:, j, :], y[:, j, k, :], w[:, :, k, :],
                                                        start=(n == 0 and k == 0), stop=(n == 2 and k == KC - 1))
                        last.then_inc(out_ready, 1)

            @block.scalar
            def _(act):
                act.sem_inc(ffn_done, B2)
                with act.Fori(0, NCH // 2) as i:
                    for j in range(2):
                        act.wait_ge(out_ready, i * 2 + (j + 1))
                        nc.scalar.activation(y_hi[:, j, :, :], y_all[:, :, bass.ds((i * 2 + j) * P, P)],
                                             ACT.Copy).then_inc(y_hi_done, 1)
                        act.wait_ge(ffn_loaded[j], i * 16 + 16)
                        nc.scalar.activation(w_ffn_sb[:, i * 2 + j, :], w_i8[:, j, :].bitcast(I8), ACT.Copy).then_inc(ffn_done, 1)
                for t in range(NCH, TT):
                    act.wait_ge(out_ready, t + 1)
                    nc.scalar.activation(y_hi[:, t % 2, :, :], y_all[:, :, t * P:(t + 1) * P],
                                         ACT.Copy).then_inc(y_hi_done, 1)

            @block.vector
            def _(dve):
                dve.sem_inc(res_done, B2)
                dve.sem_inc(x1_done, B2)
                with dve.Fori(0, TT // 2) as i:
                    for j in range(2):
                        dve.wait_ge(y_hi_done, i * 2 + (j + 1))
                        nc.vector.tensor_tensor(y_lo[:, j, :, :], y_all[:, :, bass.ds((i * 2 + j) * P, P)],
                                                y_hi[:, j, :, :].bitcast(F32), ALU.subtract).then_inc(y_lo_done, 1)
                    for j in range(2):
                        n = i * 2
                        dve.wait_ge(x_loaded[j], i * 16 + 16)
                        dve.wait_ge(out_ready, n + (B2 + j + 1))
                        dve.wait_ge(x1_done, n + (j + 1))
                        nc.vector.tensor_tensor(res[:, j, :], ps_o[:, j, :], x_in[:, j, :], ALU.add).then_inc(res_done, 1)
                        dve.wait_ge(res_done, n + (B2 + j + 1))
                        nc.vector.bn_stats(stats[:, j, :], res[:, j, :]).then_inc(stats_done, 1)
                        dve.wait_ge(stats_done, n * 2 + (2 * j + 1))
                        dve.sem_inc(passed, 1)
                        nc.vector.bn_aggr(mean_var[:, j, :], stats[:, j, :]).then_inc(stats_done, 1)
                        dve.wait_ge(stats_done, n * 2 + (2 * j + 2))
                        nc.vector.tensor_scalar(var_eps[:, j:j + 1], mean_var[:, j, 1:2], LN_EPS, None,
                                                ALU.add).then_inc(var_done, 1)
                    for j in range(2):
                        dve.wait_ge(rstd_done, i * 2 + (j + 1))
                        nc.vector.tensor_scalar(x1_all[:, i * 2 + j, :], res[:, j, :], mean_var[:, j, 0:1], rstd[:, j:j + 1],
                                                ALU.subtract, ALU.mult).then_inc(x1_done, 1)


def ffn_program(nc, scales, s_down, out, x1_all, w_ffn_sb, ident, spare, x1t_hi, x1t_lo):
    with ExitStack() as ctx:
        def sb(name, shape, dt):
            return ctx.enter_context(nc.sbuf_tensor("ff_" + name, shape, dt))

        def sem(name):
            return ctx.enter_context(nc.semaphore("ff_" + name))

        s_gu = sb("s_gu", [P, 2, NO], F32)
        s_dn = sb("s_dn", [P, C], F32)
        x1_blk = spare[:, 0, :].rearrange("p (t c) -> p t c", c=C)
        x1t_hi = x1t_hi[:].rearrange("p k t c -> p k (t c)")
        x1t_lo = x1t_lo[:].rearrange("p k t c -> p k (t c)")
        gate = sb("gate", [P, 2, BLK], F32)
        fuse = sb("fuse", [P, 2, BLK], F32)
        fuse_hi = sb("fuse_hi", [P, 2, BLK], F32R)
        fuse_lo = sb("fuse_lo", [P, 2, BLK], F32R)
        z = spare[:, 1, :].rearrange("p (t c) -> p t c", c=C)
        result = spare[:, 2, :].rearrange("p (t c) -> p t c", c=C)
        stats = sb("stats2", [P, TB, 6], F32)
        mean_var = sb("mean_var2", [P, TB, 2], F32)
        var_eps = sb("var_eps2", [P, TB], F32)
        rstd = sb("rstd2", [P, TB], F32)
        half = sb("half2", [P, TB], F32)
        ps_g = ctx.enter_context(nc.psum_tensor("ff_ps_g", [P, 2, BLK], F32))
        ps_u = ctx.enter_context(nc.psum_tensor("ff_ps_u", [P, 2, BLK], F32))
        ps_d = ctx.enter_context(nc.psum_tensor("ff_ps_d", [P, TB, C], F32))

        consts_loaded, half_set, passed = sem("consts_loaded"), sem("half_set2"), sem("passed")
        blk_loaded, x1_turned, x1_hi_done, x1_lo_done = (
            sem("blk_loaded"), sem("x1_turned"), sem("x1_hi_done"), sem("x1_lo_done"))
        gate_ready, up_ready, gate_done, fuse_done, fuse_hi_done, fuse_lo_done, down_done = (
            sem("gate_ready"), sem("up_ready"), sem("gate_done"), sem("fuse_done"), sem("fuse_hi_done"),
            sem("fuse_lo_done"), sem("down_done"))
        z_scaled, z_done, stats_done, var_done, rstd_done, result_done, stored = (
            sem("z_scaled"), sem("z_done"), sem("stats_done2"), sem("var_done2"), sem("rstd_done2"),
            sem("result_done"), [sem(f"stored{t}") for t in range(TB)])
        B2 = 2

        w_gate = w_ffn_sb[:, 0:4, :]
        w_up = w_ffn_sb[:, 4:8, :]
        w_down = w_ffn_sb[:, 8:12, :].rearrange("p c (o n) -> p (c o) n", n=C)

        with nc.Block() as block:
            @block.sync
            def _(sp):
                for t in range(TB):
                    sp.sem_inc(stored[t], 16)
                sp.dma_start(s_gu[:], scales).then_inc(consts_loaded, 16)
                sp.dma_start(s_dn[:], s_down.unsqueeze(0).to_broadcast([P, C])).then_inc(consts_loaded, 16)
                with sp.Fori(0, NB) as b:
                    sp.wait_ge(x1_turned, b * KC + KC)
                    sp.dma_start(x1_blk, x1_all[:, bass.ds(b * TB, TB), :]).then_inc(blk_loaded, 16)
                    for t in range(TB):
                        sp.wait_ge(result_done, b * TB + (TB + t + 1))
                        sp.dma_start(out[b * TB + t], result[:, t, :]).then_inc(stored[t], 16)
                for t in range(TB):
                    sp.wait_ge(stored[t], 16 * (NB + 1))

            @block.gpsimd
            def _(pool):
                pool.sem_inc(fuse_lo_done, B2)
                nc.gpsimd.memset(half[:], -0.5).then_inc(half_set, 1)
                pool.wait_ge(half_set, 1)
                with pool.Fori(0, NB) as b:
                    for o in range(NO):
                        pool.wait_ge(fuse_hi_done, b * NO + (o + 1))
                        pool.wait_ge(down_done, b * NO + (o + 1))
                        nc.gpsimd.tensor_tensor(fuse_lo[:, o % 2, :], fuse[:, o % 2, :],
                                                fuse_hi[:, o % 2, :].bitcast(F32), ALU.subtract).then_inc(fuse_lo_done, 1)
                    pool.wait_ge(var_done, b + 1)
                    nc.gpsimd.tensor_tensor(rstd[:], var_eps[:], half[:], ALU.pow).then_inc(rstd_done, 1)

            @block.tensor
            def _(pe):
                pe.sem_inc(x1_turned, KC)
                pe.sem_inc(down_done, B2)
                with pe.Fori(0, NB) as b:
                    pe.wait_ge(blk_loaded, b * 16 + 16)
                    pe.wait_ge(z_scaled, b * TB + TB)
                    for k in range(KC):
                        for t in range(TB):
                            last = nc.tensor.transpose(ps_d[:, k, t * P:(t + 1) * P],
                                                       x1_blk[:, t, k * P:(k + 1) * P], ident[:])
                        last.then_inc(x1_turned, 1)

                    def down(o):
                        pe.wait_ge(fuse_hi_done, b * NO + (o + 1))
                        for n, f in enumerate((fuse_hi, fuse_lo)):
                            if n == 1:
                                pe.wait_ge(fuse_lo_done, b * NO + (B2 + o + 1))
                            for t in range(TB):
                                last = nc.tensor.matmul(ps_d[:, t, :], f[:, o % 2, t * P:(t + 1) * P], w_down[:, o, :],
                                                        start=(o == 0 and n == 0), stop=(o == NO - 1 and n == 1))
                        last.then_inc(down_done, 1)

                    for o in range(NO):
                        for ps, w, ready, free in ((ps_g, w_gate, gate_ready, gate_done), (ps_u, w_up, up_ready, fuse_done)):
                            pe.wait_ge(free, b * NO + (o + 1))
                            for n, m in enumerate((x1t_hi, x1t_lo)):
                                for k in range(KC):
                                    if o == 0 and ps is ps_g:
                                        pe.wait_ge((x1_hi_done, x1_lo_done)[n], b * KC + (k + 1))
                                    last = nc.tensor.matmul(ps[:, o % 2, :], w[:, k, o * P:(o + 1) * P], m[:, k, :],
                                                            start=(n == 0 and k == 0), stop=(n == 1 and k == KC - 1))
                            last.then_inc(ready, 1)
                        if o >= 1:
                            down(o - 1)
                    down(NO - 1)

            @block.scalar
            def _(act):
                act.sem_inc(gate_done, B2)
                act.wait_ge(consts_loaded, 32)
                with act.Fori(0, NB) as b:
                    for k in range(KC):
                        act.wait_ge(x1_turned, b * KC + (KC + k + 1))
                        nc.scalar.activation(x1t_hi[:, k, :], ps_d[:, k, :], ACT.Copy).then_inc(x1_hi_done, 1)

                    def fuse_high(o):
                        act.wait_ge(fuse_done, b * NO + (B2 + o + 1))
                        act.wait_ge(down_done, b * NO + (o + 1))
                        nc.scalar.activation(fuse_hi[:, o % 2, :], fuse[:, o % 2, :], ACT.Copy).then_inc(fuse_hi_done, 1)

                    for o in range(NO):
                        act.wait_ge(gate_ready, b * NO + (o + 1))
                        act.wait_ge(fuse_done, b * NO + (o + 1))
                        nc.scalar.activation(gate[:, o % 2, :], ps_g[:, o % 2, :], ACT.Silu,
                                             scale=s_gu[:, 0, o:o + 1]).then_inc(gate_done, 1)
                        fuse_high(o)

            @block.vector
            def _(dve):
                dve.sem_inc(z_scaled, TB)
                dve.sem_inc(fuse_done, B2)
                dve.sem_inc(result_done, TB)
                dve.wait_ge(consts_loaded, 32)
                with dve.Fori(0, NB) as b:
                    for k in range(KC):
                        dve.wait_ge(x1_hi_done, b * KC + (k + 1))
                        nc.vector.tensor_tensor(x1t_lo[:, k, :], ps_d[:, k, :], x1t_hi[:, k, :].bitcast(F32),
                                                ALU.subtract).then_inc(x1_lo_done, 1)
                    for o in range(NO):
                        dve.wait_ge(up_ready, b * NO + (o + 1))
                        dve.wait_ge(gate_done, b * NO + (B2 + o + 1))
                        dve.wait_ge(fuse_lo_done, b * NO + (o + 1))
                        nc.vector.scalar_tensor_tensor(fuse[:, o % 2, :], ps_u[:, o % 2, :], s_gu[:, 1, o:o + 1],
                                                       gate[:, o % 2, :], ALU.mult, ALU.mult).then_inc(fuse_done, 1)
                    dve.wait_ge(down_done, b * NO + (B2 + NO))
                    dve.wait_ge(result_done, b * TB + TB)
                    for t in range(TB):
                        nc.vector.tensor_tensor(z[:, t, :], ps_d[:, t, :], s_dn[:], ALU.mult).then_inc(z_scaled, 1)
                    for t in range(TB):
                        dve.wait_ge(z_scaled, b * TB + (TB + t + 1))
                        nc.vector.tensor_tensor(z[:, t, :], z[:, t, :], x1_all[:, b * TB + t, :], ALU.add).then_inc(z_done, 1)
                    for t in range(TB):
                        dve.wait_ge(z_done, b * TB + (t + 1))
                        nc.vector.bn_stats(stats[:, t, :], z[:, t, :]).then_inc(stats_done, 1)
                    dve.wait_ge(stats_done, b * (2 * TB) + TB)
                    dve.sem_inc(passed, 1)
                    for t in range(TB):
                        nc.vector.bn_aggr(mean_var[:, t, :], stats[:, t, :]).then_inc(stats_done, 1)
                    dve.wait_ge(stats_done, b * (2 * TB) + 2 * TB)
                    nc.vector.tensor_scalar(var_eps[:], mean_var[:, :, 1], LN_EPS, None, ALU.add).then_inc(var_done, 1)
                    dve.wait_ge(rstd_done, b + 1)
                    for t in range(TB):
                        dve.wait_ge(stored[t], b * 16 + 16)
                        nc.vector.tensor_scalar(result[:, t, :], z[:, t, :], mean_var[:, t, 0:1], rstd[:, t:t + 1],
                                                ALU.subtract, ALU.mult).then_inc(result_done, 1)


def build(nc, x, w_qkv, w_o, rope, w_ffn, scales, s_down, out):
    xt = x.rearrange("(t p) c -> t p c", p=P)
    with ExitStack() as ctx:
        def sb(name, shape, dt):
            return ctx.enter_context(nc.sbuf_tensor(name, shape, dt))

        ident = sb("ident", [P, P], F32)
        y_all = sb("y_all", [P, G, T], F32)
        parts = nc.dram_tensor("parts", (2, G, NB, P, 2, BLK), F32, kind="Internal").ap()
        wo_hi = sb("wo_hi", [P, G, KC, P], F32R)
        wo_lo = sb("wo_lo", [P, G, KC, P], F32R)
        with nc.sbuf_tensor("v_all", [P, T // P, C], F32) as v_all:
            project_program(nc, x.rearrange("(b t p) c -> b p t c", p=P, t=TB), w_qkv, w_o, rope, parts, v_all,
                            wo_hi, wo_lo, ident)
            attention_program(nc, parts, y_all, v_all, ident)
        x1_all = sb("x1_all", [P, T // P, C], F32)
        w_ffn_sb = sb("w_ffn_sb", [P, NCH, INTER], F32R)
        output_program(nc, xt, wo_hi, wo_lo, w_ffn, y_all, x1_all, w_ffn_sb)
        ffn_program(nc, scales, s_down, out.rearrange("(t p) c -> t p c", p=P), x1_all, w_ffn_sb, ident, y_all,
                    wo_hi, wo_lo)


def kernel(**inputs):
    import numpy as np
    import concourse.bacc as bacc
    from concourse.bass_utils import run_bass_kernel_spmd

    w = {n: np.asarray(inputs["L0_attn_w_" + n]) for n in "qkvo"}
    gate, up, down = (np.asarray(inputs["L0_ffn_w_" + n]) for n in ("gate", "up", "down"))
    inv_freq = np.float32(1) / np.power(np.float32(10000), np.arange(HD // 2, dtype=np.float32) / np.float32(HD // 2))
    angle = np.outer(inv_freq, np.arange(T, dtype=np.float32)).astype(np.float32)
    cos, sin = np.cos(angle), np.sin(angle)
    rope = np.stack([np.concatenate([cos, cos]), np.concatenate([-sin, sin])], axis=1)
    rope = np.tile(rope, (HG, 1, 1))
    arrays = {
        "x": np.asarray(inputs["L0_attn_x"]).reshape(T, C),
        "w_qkv": np.concatenate([w["q"], w["k"], w["v"]]).reshape(3 * G, P, C),
        "w_o": w["o"].reshape(G, P, C),
        "rope": rope.reshape(P, 2, NB, BLK).transpose(2, 0, 1, 3),
        "w_ffn": np.concatenate([gate.reshape(4, P, INTER), up.reshape(4, P, INTER),
                                 down.reshape(4, 4, P, C).transpose(0, 2, 1, 3).reshape(4, P, INTER)]),
        "scales": np.stack([np.asarray(inputs["L0_ffn_s_gate"]).reshape(NO, P),
                            np.asarray(inputs["L0_ffn_s_up"]).reshape(NO, P)]).transpose(2, 0, 1),
        "s_down": np.asarray(inputs["L0_ffn_s_down"]),
    }
    arrays = {n: np.ascontiguousarray(a) for n, a in arrays.items()}
    arrays["w_ffn"] = arrays["w_ffn"].view(np.int32)
    nc = bacc.Bacc("TRN2", target_bir_lowering=False, num_devices=1)
    args = {n: nc.dram_tensor(n, a.shape, mybir.dt.from_np(a.dtype), kind="ExternalInput").ap() for n, a in arrays.items()}
    out = nc.dram_tensor("out", (T, C), F32, kind="ExternalOutput").ap()
    build(nc, **args, out=out)
    r = run_bass_kernel_spmd(nc, [arrays], core_ids=[0])
    return r.results[0]["out"].reshape(1, T, C)
```

```python
from contextlib import ExitStack

import concourse.bass as bass
from concourse import mybir

ALU = mybir.AluOpType
ACT = mybir.ActivationFunctionType
AX_X = mybir.AxisListType.X
F32 = mybir.dt.float32
F32R = mybir.dt.float32r
BF16 = mybir.dt.bfloat16
I8 = mybir.dt.int8
I32 = mybir.dt.int32

P = 128
T = 2048
C = 512
INTER = 2048
HD = 32
KC = C // P
HG = P // HD
G = C // P
BLK = 512
NB = T // BLK
TB = BLK // P
QGRP = 128
SCALE = float(HD) ** -0.5
W_EPS = 1e-8
LN_EPS = 1e-5
LOWEST = -3.0e38
MROW = 3 * HD
NCH = 12
NO = INTER // P
NORM_AT = (0, 4, 8, 10)




QSTEPS = 3


def quantize_tile(dve, nc, raw, quant, sign, small, step, base, sign_done, nth, signs):
    nc.vector.tensor_reduce(small[:, 0:4], raw.rearrange("p (g c) -> p g c", c=QGRP), AX_X, ALU.add,
                            apply_absolute_value=True).then_inc(step, 1)
    dve.wait_ge(step, base + 1)
    nc.vector.tensor_scalar(small[:, 4:8], small[:, 0:4], 1.0 / QGRP, W_EPS, ALU.mult, ALU.max).then_inc(step, 1)
    dve.wait_ge(step, base + 2)
    dve.wait_ge(sign_done, nth)
    for g in range(C // QGRP):
        cols = slice(g * QGRP, (g + 1) * QGRP)
        last = nc.vector.tensor_scalar(quant[:, cols], quant[:, cols], small[:, 4 + g:5 + g], None, ALU.is_gt)
    last.then_inc(step, 1)
    dve.wait_ge(step, base + 3)
    for g in range(C // QGRP):
        cols = slice(g * QGRP, (g + 1) * QGRP)
        last = nc.vector.scalar_tensor_tensor(quant[:, cols], quant[:, cols], small[:, 4 + g:5 + g], sign[:, cols],
                                              ALU.mult, ALU.mult)
    last.then_inc(signs, 1)


def project_program(nc, x, w_qkv, w_o, rope, parts, v_all, wo_hi, wo_lo, ident, spare):
    NT = 3 * G
    NP = 2 * G + TB
    NR = 2 * G
    with ExitStack() as ctx:
        def sb(name, shape, dt):
            return ctx.enter_context(nc.sbuf_tensor("pj_" + name, shape, dt))

        def sem(name):
            return ctx.enter_context(nc.semaphore("pj_" + name))

        wt_hi = sb("wt_hi", [P, NT, KC, P], F32R)
        wt_lo = sb("wt_lo", [P, NT, KC, P], F32R)
        w_raw = spare[:, 0, :].rearrange("p (j c) -> p j c", c=C)
        w_q = spare[:, 1:3, :].rearrange("p a (j s c) -> p (a j) s c", s=2, c=C)
        w_small = sb("w_small", [P, 4, 8], F32)
        x_nat = sb("x_nat", [P, TB, C], F32)
        xt_hi = sb("xt_hi", [P, KC, BLK], F32R)
        xt_lo = sb("xt_lo", [P, KC, BLK], F32R)
        rope_t = sb("rope_t", [P, 2, BLK], F32)
        proj = sb("proj", [P, 2, BLK], F32)
        turned = sb("turned", [P, 2, BLK], F32)
        by_cos = sb("by_cos", [P, 2, BLK], F32)
        rotated = sb("rotated", [P, 2, BLK], F32)
        split = sb("split", [P, 4, 2, BLK], F32R)
        ps_t = ctx.enter_context(nc.psum_tensor("pj_ps_t", [P, KC, BLK], F32))
        ps_o = ctx.enter_context(nc.psum_tensor("pj_ps_o", [P, 4, BLK], F32))

        ident_zero, ident_ready, passed = sem("ident_zero"), sem("ident_ready"), sem("passed")
        w_loaded, w_sign, wo_sign = [sem(f"w_loaded{j}") for j in range(4)], sem("w_sign"), sem("wo_sign")
        w_step, w_signs, w_sub, w_ste = sem("w_step"), sem("w_signs"), sem("w_sub"), sem("w_ste")
        w_turned, w_hi_done, w_lo_done = sem("w_turned"), sem("w_hi_done"), sem("w_lo_done")
        wo_loaded, wo_step, wo_signs, wo_sub, wo_ste = (
            sem("wo_loaded"), sem("wo_step"), sem("wo_signs"), sem("wo_sub"), sem("wo_ste"))
        wo_turned, wo_hi_done, wo_lo_done = sem("wo_turned"), sem("wo_hi_done"), sem("wo_lo_done")
        x_loaded, rope_loaded = sem("x_loaded"), sem("rope_loaded")
        x_turned, x_hi_done, x_lo_done = sem("x_turned"), sem("x_hi_done"), sem("x_lo_done")
        prod_ready, prod_copied = sem("prod_ready"), sem("prod_copied")
        turn_done, cos_done, sin_done, rope_done = sem("turn_done"), sem("cos_done"), sem("sin_done"), sem("rope_done")
        split_hi, split_lo, stored = sem("split_hi"), sem("split_lo"), [sem(f"stored{i}") for i in range(4)]
        W4, KC4, O4, R2, O1 = 4, KC, 4, 2, 1
        WO_AT = 5
        LEAD = 2
        LAG = TB

        def weight_tile(n):
            return (n + NR) % NT

        def product(p, first):
            if first:
                return ("v", p) if p < TB else ("r", p - TB)
            return ("r", p) if p < NR else ("v", p - NR)

        def blocks(eng, first_block, body):
            first_block()
            with eng.Fori(1, NB) as b:
                body(b)

        with nc.Block() as block:
            @block.sync
            def _(sp):
                def load_x(b):
                    sp.wait_ge(x_turned, b * KC + KC4)
                    sp.dma_start(x_nat[:], x[b]).then_inc(x_loaded, 16)

                def load_wo(b):
                    sp.wait_ge(wo_ste, b + O1)
                    sp.dma_start(w_raw[:, 0, :], w_o[b]).then_inc(wo_loaded, 16)

                def load_rope(b):
                    sp.wait_ge(rope_done, b * NR + R2)
                    sp.dma_start(rope_t[:], rope[b]).then_inc(rope_loaded, 16)

                def body(b, first=False, last=False):
                    if first:
                        load_x(b + 1)
                    for i in range(NR):
                        if i == 4 and not last:
                            if not first:
                                load_x(b + 1)
                            load_wo(b + 1)
                        sp.wait_ge(split_lo, b * NR + (O4 + i + 1))
                        sp.dma_start(parts[i // G, i % G, b], split[:, i % 4, :, :].bitcast(F32)).then_inc(stored[i % 4], 16)
                    if not last:
                        load_rope(b + 1)

                for s in stored:
                    sp.sem_inc(s, 16)
                for n in range(NT):
                    sp.wait_ge(w_ste, n + 1)
                    sp.dma_start(w_raw[:, n % 4, :], w_qkv[weight_tile(n)]).then_inc(w_loaded[n % 4], 16)
                    if n == LEAD - 1:
                        load_x(0)
                load_rope(0)
                sp.wait_ge(w_turned, W4 + NT - 3)
                load_wo(0)
                body(0, first=True)
                with sp.Fori(1, NB - 1) as b:
                    body(b)
                body(NB - 1, last=True)
                for s in stored:
                    sp.wait_ge(s, 16 * (NB * NR // 4 + 1))

            @block.gpsimd
            def _(pool):
                def straight_through(j, signs, sub, n, ste):
                    pool.wait_ge(signs, n)
                    nc.gpsimd.tensor_tensor(w_q[:, j, 1, :], w_q[:, j, 0, :], w_raw[:, j, :],
                                            ALU.subtract).then_inc(sub, 1)
                    pool.wait_ge(sub, n)
                    nc.gpsimd.tensor_tensor(w_q[:, j, 0, :], w_raw[:, j, :], w_q[:, j, 1, :],
                                            ALU.add).then_inc(ste, 1)

                pool.sem_inc(w_ste, W4)
                pool.sem_inc(wo_ste, O1)
                pool.sem_inc(split_lo, O4)
                nc.gpsimd.memset(ident[:], 0.0).then_inc(ident_zero, 1)
                pool.wait_ge(ident_zero, 1)
                nc.gpsimd.affine_select(out=ident[:], in_=ident[:], compare_op=ALU.not_equal, fill=1.0, base=0,
                                        pattern=[[-1, P]], channel_multiplier=1).then_inc(ident_ready, 1)

                def by_cosine(b, i, p):
                    pool.wait_ge(prod_copied, b * NP + (O4 + p + 1))
                    pool.wait_ge(rope_done, b * NR + (i + 1))
                    nc.gpsimd.tensor_tensor(by_cos[:, i % 2, :], proj[:, i % 2, :], rope_t[:, 0, :],
                                            ALU.mult).then_inc(cos_done, 1)

                def low(b, i):
                    pool.wait_ge(split_hi, b * NR + (i + 1))
                    nc.gpsimd.tensor_tensor(split[:, i % 4, 1, :], rotated[:, i % 2, :],
                                            split[:, i % 4, 0, :].bitcast(F32), ALU.subtract).then_inc(split_lo, 1)

                def first_block():
                    straight_through(0, w_signs, w_sub, 1, w_ste)
                    for n in range(NT + LAG + 3):
                        if n + 1 < NT:
                            straight_through((n + 1) % 4, w_signs, w_sub, n + 2, w_ste)
                        if n == NT:
                            straight_through(0, wo_signs, wo_sub, 1, wo_ste)
                        i = n - LAG - TB - 1
                        if i == 0:
                            pool.wait_ge(rope_loaded, 16)
                        if 0 <= i < NR:
                            by_cosine(0, i, i + TB)
                        if 2 <= i < NR + 2:
                            low(0, i - 2)

                def body(b):
                    straight_through(0, wo_signs, wo_sub, b + 1, wo_ste)
                    pool.wait_ge(rope_loaded, b * 16 + 16)
                    for i in range(NR):
                        by_cosine(b, i, i)
                        if i:
                            low(b, i - 1)
                    low(b, NR - 1)

                blocks(pool, first_block, body)

            @block.tensor
            def _(pe):
                pe.sem_inc(w_turned, W4)
                pe.sem_inc(x_turned, KC4)
                pe.sem_inc(wo_turned, O1)
                pe.wait_ge(ident_ready, 1)

                def turn_tokens(b):
                    pe.wait_ge(x_loaded, b * 16 + 16)
                    pe.wait_ge(wo_lo_done, b + O1)
                    for k in range(KC):
                        pe.wait_ge(x_lo_done, b * KC + (k + 1))
                        for t in range(TB):
                            last = nc.tensor.transpose(ps_t[:, k, t * P:(t + 1) * P],
                                                       x_nat[:, t, k * P:(k + 1) * P], ident[:])
                        last.then_inc(x_turned, 1)

                def turn_weights(j, done):
                    for k in range(KC):
                        last = nc.tensor.transpose(ps_t[:, j, k * P:(k + 1) * P], w_q[:, j, 0, k * P:(k + 1) * P], ident[:])
                    last.then_inc(done, 1)

                def multiply(b, p, first=False):
                    pe.wait_ge(prod_copied, b * NP + (p + 1))
                    kind, i = product(p, first)
                    if kind == "r":
                        terms = [(wt_hi, xt_hi), (wt_hi, xt_lo), (wt_lo, xt_hi)]
                    else:
                        terms = [(xt_hi, wt_hi), (xt_lo, wt_hi), (xt_hi, wt_lo)]
                    for n, (w, m) in enumerate(terms):
                        for k in range(KC):
                            if p == 0 and n < 2:
                                part_done = (x_hi_done, x_lo_done)[n]
                                pe.wait_ge(part_done, b * KC + ((KC4 if n == 1 else 0) + k + 1))
                            if kind == "r":
                                lhs, rhs = w[:, i, k, :], m[:, k, :]
                            else:
                                lhs, rhs = w[:, k, i * P:(i + 1) * P], m[:, 2 * G:3 * G, k, :]
                            last = nc.tensor.matmul(ps_o[:, p % 4, :], lhs, rhs,
                                                    start=(n == 0 and k == 0), stop=(n == 2 and k == KC - 1))
                    last.then_inc(prod_ready, 1)

                def first_block():
                    turn_tokens(0)
                    for n in range(NT + LAG):
                        if n < NT:
                            pe.wait_ge(w_ste, W4 + n + 1)
                            pe.wait_ge(w_lo_done, n + 1)
                            if n < KC:
                                pe.wait_ge(x_lo_done, KC4 + n + 1)
                            turn_weights(n % 4, w_turned)
                        if n == NT + 2:
                            pe.wait_ge(wo_ste, O1 + 1)
                            turn_weights(0, wo_turned)
                        if n >= LAG:
                            pe.wait_ge(w_lo_done, W4 + max(TB, n - LAG + 1))
                            multiply(0, n - LAG, True)

                def body(b):
                    turn_tokens(b)
                    for p in range(NP):
                        multiply(b, p)
                        if p == WO_AT:
                            pe.wait_ge(wo_ste, b + (O1 + 1))
                            turn_weights(0, wo_turned)

                blocks(pe, first_block, body)

            @block.scalar
            def _(act):
                act.sem_inc(prod_copied, O4)

                def magnitude_and_sign(j, done):
                    nc.scalar.activation(w_q[:, j, 0, :], w_raw[:, j, :], ACT.Abs, scale=2.0)
                    nc.scalar.activation(w_q[:, j, 1, :], w_raw[:, j, :], ACT.Sign).then_inc(done, 1)

                def sign(n):
                    act.wait_ge(w_loaded[n % 4], 16 * (n // 4 + 1))
                    act.wait_ge(w_turned, n + 1)
                    magnitude_and_sign(n % 4, w_sign)

                def sign_wo(b):
                    act.wait_ge(wo_loaded, b * 16 + 16)
                    act.wait_ge(wo_turned, b + O1)
                    magnitude_and_sign(0, wo_sign)

                def high_weights(n):
                    act.wait_ge(w_turned, W4 + n + 1)
                    nc.scalar.activation(wt_hi[:, weight_tile(n), :, :], ps_t[:, n % 4, :].rearrange("p (k c) -> p k c", c=P),
                                         ACT.Copy).then_inc(w_hi_done, 1)

                def high_wo(b):
                    act.wait_ge(wo_turned, b + (O1 + 1))
                    nc.scalar.activation(wo_hi[:, b, :, :], ps_t[:, 0, :].rearrange("p (k c) -> p k c", c=P),
                                         ACT.Copy).then_inc(wo_hi_done, 1)

                def high_tokens(b):
                    for k in range(KC):
                        act.wait_ge(x_turned, b * KC + (KC4 + k + 1))
                        nc.scalar.activation(xt_hi[:, k, :], ps_t[:, k, :], ACT.Copy).then_inc(x_hi_done, 1)

                def copy(b, p, first=False):
                    act.wait_ge(prod_ready, b * NP + (p + 1))
                    kind, i = product(p, first)
                    if kind == "r":
                        act.wait_ge(rope_done, b * NR + (i + 1))
                        nc.scalar.activation(proj[:, i % 2, :], ps_o[:, p % 4, :], ACT.Copy).then_inc(prod_copied, 1)
                    else:
                        nc.scalar.activation(v_all[:, b * TB + i, :], ps_o[:, p % 4, :], ACT.Copy).then_inc(prod_copied, 1)

                def high(b, i):
                    act.wait_ge(rope_done, b * NR + (R2 + i + 1))
                    act.wait_ge(stored[i % 4], b * (16 * NR // 4) + 16 * (i // 4 + 1))
                    nc.scalar.activation(split[:, i % 4, 0, :], rotated[:, i % 2, :], ACT.Copy).then_inc(split_hi, 1)

                def first_block():
                    for n in range(LEAD):
                        sign(n)
                    high_tokens(0)
                    for n in range(NT + LAG + 3):
                        if n + LEAD < NT:
                            sign(n + LEAD)
                        if n == NT - 1:
                            sign_wo(0)
                        if n < NT:
                            high_weights(n)
                        if n == NT + 3:
                            high_wo(0)
                        p = n - LAG - 1
                        if 0 <= p < NP:
                            copy(0, p, True)
                        if TB + 2 <= p:
                            high(0, p - TB - 2)

                def body(b):
                    high_tokens(b)
                    sign_wo(b)
                    for p in range(NP):
                        copy(b, p)
                        if 1 <= p <= NR:
                            high(b, p - 1)
                        if p == WO_AT + 1:
                            high_wo(b)

                blocks(act, first_block, body)

            @block.vector
            def _(dve):
                dve.sem_inc(w_lo_done, W4)
                dve.sem_inc(wo_lo_done, O1)
                dve.sem_inc(x_lo_done, KC4)
                dve.sem_inc(rope_done, R2)
                swap = [(r + HD // 2) % HD for r in range(HD)]

                def quantize(n):
                    j = n % 4
                    dve.wait_ge(w_loaded[j], 16 * (n // 4 + 1))
                    quantize_tile(dve, nc, w_raw[:, j, :], w_q[:, j, 0, :], w_q[:, j, 1, :], w_small[:, j],
                                  w_step, n * QSTEPS, w_sign, n + 1, w_signs)

                def quantize_wo(b):
                    dve.wait_ge(wo_loaded, b * 16 + 16)
                    quantize_tile(dve, nc, w_raw[:, 0, :], w_q[:, 0, 0, :], w_q[:, 0, 1, :], w_small[:, 0],
                                  wo_step, b * QSTEPS, wo_sign, b + 1, wo_signs)

                def low_weights(n):
                    dve.wait_ge(w_hi_done, n + 1)
                    nc.vector.tensor_tensor(wt_lo[:, weight_tile(n), :, :], ps_t[:, n % 4, :].rearrange("p (k c) -> p k c", c=P),
                                            wt_hi[:, weight_tile(n), :, :].bitcast(F32), ALU.subtract).then_inc(w_lo_done, 1)

                def low_wo(b):
                    dve.wait_ge(wo_hi_done, b + 1)
                    nc.vector.tensor_tensor(wo_lo[:, b, :, :], ps_t[:, 0, :].rearrange("p (k c) -> p k c", c=P),
                                            wo_hi[:, b, :, :].bitcast(F32), ALU.subtract).then_inc(wo_lo_done, 1)

                def low_tokens(b):
                    for k in range(KC):
                        dve.wait_ge(x_hi_done, b * KC + (k + 1))
                        nc.vector.tensor_tensor(xt_lo[:, k, :], ps_t[:, k, :], xt_hi[:, k, :].bitcast(F32),
                                                ALU.subtract).then_inc(x_lo_done, 1)

                def rotate(b, i, p):
                    dve.wait_ge(prod_copied, b * NP + (O4 + p + 1))
                    dve.sem_inc(passed, 1)
                    nc.vector.stream_shuffle(turned[:, i % 2, :], proj[:, i % 2, :], swap).then_inc(turn_done, 1)
                    dve.wait_ge(turn_done, b * NR + (i + 1))
                    nc.vector.tensor_tensor(turned[:, i % 2, :], turned[:, i % 2, :], rope_t[:, 1, :],
                                            ALU.mult).then_inc(sin_done, 1)
                    dve.wait_ge(sin_done, b * NR + (i + 1))
                    dve.wait_ge(cos_done, b * NR + (i + 1))
                    if i >= 2:
                        dve.wait_ge(split_lo, b * NR + (O4 + i - 1))
                    nc.vector.tensor_tensor(rotated[:, i % 2, :], by_cos[:, i % 2, :], turned[:, i % 2, :],
                                            ALU.add).then_inc(rope_done, 1)

                def first_block():
                    for n in range(LEAD):
                        quantize(n)
                    low_tokens(0)
                    for n in range(NT + LAG + 3):
                        if n + LEAD < NT:
                            quantize(n + LEAD)
                        if n == NT - 1:
                            quantize_wo(0)
                        if n < NT:
                            low_weights(n)
                        i = n - LAG - TB - 1
                        if i == 0:
                            dve.wait_ge(rope_loaded, 16)
                        if 0 <= i < NR:
                            rotate(0, i, i + TB)
                        if n == NT + 3:
                            low_wo(0)

                def body(b):
                    low_tokens(b)
                    quantize_wo(b)
                    dve.wait_ge(rope_loaded, b * 16 + 16)
                    for i in range(NR):
                        rotate(b, i, i)
                        if i == WO_AT + 2:
                            low_wo(b)

                blocks(dve, first_block, body)


def units(b):
    return ([(j, 1, qt, c) for c in range(b) for qt in range(TB) for j in range(HG)]
            + [(j, n, qt, b) for qt, n in ((0, 4), (1, 2), (2, 1), (3, 1)) for j in range(0, HG, n)])


def unit_width(b, unit):
    return BLK if unit[3] < b else (unit[2] + 1) * P


AU = [len(units(b)) for b in range(NB)]
KT = [TB * (b + 1) for b in range(NB)]
NA, NK = sum(AU), sum(KT)
CUM_K = [sum(KT[:b]) for b in range(NB + 1)]
RING = 4
S3 = 3
U3 = 3
HOLD = 8.0
MAXIMA = (2, 3, 0, 1)
ORDINAL = {m: n for n, m in enumerate(MAXIMA)}


def block_tiles(b):
    full, diagonal = KT[b] - TB, TB
    return sorted(range(KT[b]), key=lambda i: i if i < full else (i - full + 0.5) * full / diagonal - 0.5 if full else i)


TILES = [(b, i) for b in range(NB) for i in block_tiles(b)]
DIAGONAL = [i >= KT[b] - TB for b, i in TILES]
LAST_USE = {c: max(t for t, (b, i) in enumerate(TILES) if i // TB == c) for c in range(NB)}
FIRST_USE = {c: min(t for t, (b, i) in enumerate(TILES) if i // TB == c) for c in range(NB)}


def first_query(t):
    b, i = TILES[t]
    return max(0, i - (KT[b] - TB)) * P


def masks_until(t):
    return 2 * sum(DIAGONAL[:t + 1])


def pass_order(last):
    SIGNAL, LOAD = 0.2, 5.0
    scores = [("scores", t, j) for t in range(NK) for j in range(HG)]
    maxima = []
    for m in MAXIMA[:2] if last else MAXIMA:
        maxima += [("max", m, u) for u in range(AU[m])] + [("turn", m)]
    products = []
    for t in range(NK):
        products += [("sums", t), ("values", t)]
        if t + 1 in CUM_K:
            products[-1:] = [("fold", TILES[t][0]), ("values", t), ("copy", TILES[t][0])]
    order = []
    pe = act = vector = pool = 0.0
    score_free, unit_free = [0.0] * S3, [0.0] * U3
    at = {("placed", 0): 0.0, ("placed", 1): 0.0, ("loaded", 2, 0): 0.0, ("loaded", 3, 0): LOAD, "turned": 0.0}
    chain, waiting, added, folds = 0.0, None, set(), set()
    later = []
    never = 1e9

    def width(t):
        return 1 - first_query(t) / BLK

    while scores or maxima or products:
        while later and later[0][0] <= max(vector, pe):
            vector = max(vector, later[0][0]) + 0.8
            order.append(later.pop(0)[1])
        while products and (products[0][0] == "sums" and products[0][1] in added
                            or products[0][0] == "fold" and products[0][1] not in folds):
            products.pop(0)
        starts = []
        if scores:
            t = scores[0][1]
            behind = next(p[1] for p in products if p[0] == "values")
            ready = score_free[0] if t - behind < RING else never
            if t in CUM_K:
                ready = max(ready, at.get(("placed", TILES[t][0]), never))
            starts.append((ready, 1, scores))
        if maxima:
            step = maxima[0]
            if step[0] == "turn":
                ready = at["max_ready"]
            else:
                m, c = step[1], units(step[1])[step[2]][3]
                ready = at.get(("loaded", m, c if m < 2 else 0), never)
            starts.append((max(ready, unit_free[0]), 0, maxima))
        if products:
            kind, t = products[0]
            ready = 0.0
            if kind == "sums" or kind == "values" and t in added:
                ready = at.get(("mask", t) if DIAGONAL[t] else ("exp", t, HG - 1), never)
                if t in CUM_K:
                    ready = max(ready, at["turned"])
            elif kind == "fold":
                ready = chain
            starts.append((ready, 2, products))
        chosen = min(((max(pe, r + SIGNAL), rank), n) for n, (r, rank, _) in enumerate(starts))
        pe, steps = chosen[0][0], starts[chosen[1]][2]
        soon = next((max(pe, r + SIGNAL) for r, _, those in starts if those is maxima), never)
        step = steps.pop(0)
        order.append(step)
        kind, t = step[0:2]
        if kind == "turn":
            pe += 0.5
            act = max(act, pe + SIGNAL) + 1.8
            at["placed", t] = act
            unit_free = unit_free[1:] + [act]
        elif kind == "max":
            m, u = step[1:]
            unit = units(m)[u]
            w = unit[1] * unit_width(m, unit) / BLK
            pe += 0.02 + 0.22 * w + (0 if unit[3] < m else 0.07 * unit[1])
            vector = max(vector, pe + SIGNAL) + 0.08 + 0.54 * w
            unit_free = unit_free[1:] + [vector]
            if u == AU[m] - 1:
                vector += 0.6
                at["max_ready"] = vector
                order.append(("finish", m))
        elif kind == "scores":
            pe += 0.22 * width(t)
            act = max(act, pe + SIGNAL) + 0.07 + 0.43 * width(t)
            score_free = score_free[1:] + [act]
            at["exp", t, step[2]] = act
            b = TILES[t][0]
            if DIAGONAL[t] and step[2] % 2:
                pool = max(pool, act + SIGNAL) + 0.4
                at["mask", t] = pool
            elif step[2] == HG - 1 and t not in CUM_K and not DIAGONAL[t] and t < CUM_K[b + 1] - 3:
                start = max(act + SIGNAL, chain)
                by_vector, by_pool = max(vector, start) + 2.6, max(pool, start) + 5.1
                name, done = ("vector", by_vector) if soon > act + 3 and by_vector <= by_pool else ("gpsimd", by_pool)
                if b in folds:
                    take = done <= act + HOLD
                else:
                    take = ("sums", waiting) in products and done <= at["exp", waiting, HG - 1] + HOLD
                if take:
                    order.append(("add", t, None if b in folds else waiting, name))
                    added |= {t} if b in folds else {t, waiting}
                    folds.add(b)
                    chain, waiting = done + SIGNAL, None
                    if name == "vector":
                        vector = done
                    else:
                        pool = done
                elif b not in folds:
                    waiting = t
            elif step[2] == HG - 1:
                waiting = None
        elif kind == "copy":
            vector = max(vector, pe + SIGNAL) + 0.6
            act = max(act, pe + SIGNAL) + 0.5
            at["turned"] = max(vector, act)
            later += [(vector + 0.7, ("invert", t)), (vector + 1.4, ("scale", t))]
        elif kind == "fold":
            pe += 1.03
            chain = pe + SIGNAL
        else:
            pe += 0.17 + 0.86 * width(t)
            if kind == "values":
                for c in range(2):
                    if t == LAST_USE[c]:
                        at["loaded", c, c] = at["loaded", 1 - c, c] = pe + LOAD
    return order + [step for _, step in later]


def add_numbers(order):
    numbers = {}
    for n, (_, t, before, _) in enumerate([step for step in order if step[0] == "add"], 1):
        numbers[t] = n
        if before is not None:
            numbers[before] = n
    return numbers


def attention_program(nc, parts, y_all, v_all, ident):
    with ExitStack() as ctx:
        def sb(name, shape, dt):
            return ctx.enter_context(nc.sbuf_tensor("at_" + name, shape, dt))

        def sem(name):
            return ctx.enter_context(nc.semaphore("at_" + name))

        k_stack = sb("k_stack", [P, HG, T], F32R)
        q_stack = sb("q_stack", [P, NB, HG, BLK], F32R)
        v_grp = sb("v_grp", [P, T // P, P], F32)
        probs = sb("probs", [P, RING, HG, BLK], F32)
        acc = sb("acc", [P, HG, BLK], F32)
        tail = sb("tail", [P, HG], F32)
        above = sb("above", [P, P], BF16)
        ident16 = sb("ident16", [P, P], BF16)
        ones = sb("ones", [P, HD], F32)
        part_max = sb("part_max", [P, 2, TB * HG, NB], F32)
        neg_max = sb("neg_max", [P, 2, TB * HG], F32)
        neg_max_hi = sb("neg_max_hi", [P, 2, TB * HG], F32R)
        turn_in = sb("turn_in", [P, 2, TB, P], F32)
        sums_t = sb("sums_t", [P, BLK], F32)
        inv_t = sb("inv_t", [P, BLK // HD], F32)
        inv_sum = sb("inv_sum", [P, BLK], F32)
        y_raw = sb("y_raw", [P, 2, BLK], F32)
        ps_m = ctx.enter_context(nc.psum_tensor("at_ps_m", [P, U3, BLK], F32))
        ps_s = ctx.enter_context(nc.psum_tensor("at_ps_s", [P, S3, BLK], F32))
        ps_y = ctx.enter_context(nc.psum_tensor("at_ps_y", [P, BLK], F32))
        ps_l = ctx.enter_context(nc.psum_tensor("at_ps_l", [P, BLK], F32))

        const_step, consts_ready, ones_rows = sem("const_step"), sem("consts_ready"), sem("ones_rows")
        q_loaded = [sem(f"q_loaded{b}") for b in range(NB)]
        k_loaded = [sem(f"k_loaded{b}") for b in range(NB)]
        v_loaded = [sem(f"v_loaded{b}") for b in range(NB)]
        unit_ready, unit_drained = sem("unit_ready"), sem("unit_drained")
        max_step, max_ready, max_turned, max_placed = (
            sem("max_step"), sem("max_ready"), sem("max_turned"), sem("max_placed"))
        scores_ready, exp_done, masked, values_done = (
            sem("scores_ready"), sem("exp_done"), sem("masked"), sem("values_done"))
        y_copied, sums_turned, inverted, scaled, passed = (
            sem("y_copied"), sem("sums_turned"), sem("inverted"), sem("scaled"), sem("passed"))
        added, folded = sem("added"), sem("folded")
        VR, C1 = RING, 1
        NE = HG * NK
        LOADS = 16 * 3
        U0 = AU[0] + AU[1]
        PH = 2
        R0 = -(U0 + PH) % U3
        assert (NA + NB) % U3 == 0

        def passes(eng, body):
            with eng.Fori(0, G - 1) as g:
                body(g, False)
            body(G - 1, True)

        orders = {last: pass_order(last) for last in (False, True)}
        numbers = {last: add_numbers(orders[last]) for last in orders}
        NADD = sum(step[0] == "add" for step in orders[False])
        NFOLD = sum(step[0] == "fold" for step in orders[False])

        def add(eng, vector, g, last, step, folds):
            _, t, other, _ = step
            n = numbers[last][t]
            if other is None:
                eng.wait_ge(added, g * NADD + (n - 1))
                first = acc[:]
            else:
                eng.wait_ge(folded, g * NFOLD + (folds + 1))
                first = probs[:, other % RING, :, :]
            eng.wait_ge(exp_done, g * NE + (S3 + HG * (t + 1)))
            vector.tensor_tensor(acc[:], first, probs[:, t % RING, :, :], ALU.add).then_inc(added, 1)

        def before(m):
            return PH + ORDINAL[m]

        with nc.Block() as block:
            @block.gpsimd
            def _(pool):
                nc.gpsimd.memset(tail[:], 0.0).then_inc(const_step, 1)
                nc.gpsimd.memset(above[:], 0.0).then_inc(const_step, 1)
                pool.wait_ge(const_step, 2)
                for r in range(2):
                    nc.gpsimd.affine_select(out=tail[:], in_=tail[:], compare_op=ALU.not_equal, fill=1.0,
                                            base=-MROW - r, pattern=[[-2, HG]], channel_multiplier=1).then_inc(const_step, 1)
                    pool.wait_ge(const_step, 3 + r)
                nc.gpsimd.memset(turn_in[:], 0.0).then_inc(consts_ready, 1)
                nc.gpsimd.memset(ones[:], 1.0).then_inc(consts_ready, 1)
                nc.gpsimd.affine_select(out=above[:], in_=above[:], compare_op=ALU.is_ge, fill=LOWEST, base=0,
                                        pattern=[[-1, P]], channel_multiplier=1).then_inc(consts_ready, 1)
                nc.gpsimd.tensor_copy(ident16[:], ident[:]).then_inc(consts_ready, 1)

                def body(g, last):
                    folds = 0
                    for step in orders[last]:
                        folds += step[0] == "fold"
                        if step[0] == "add" and step[3] == "gpsimd":
                            add(pool, nc.gpsimd, g, last, step, folds)
                        if step[0] == "scores":
                            _, t, j = step
                            if not DIAGONAL[t] or j % 2 == 0:
                                continue
                            pool.wait_ge(exp_done, g * NE + (S3 + HG * t + j + 1))
                            pool.sem_inc(passed, 1)
                            lo = first_query(t)
                            tri = probs[:, t % RING, j - 1:j + 1, lo:lo + P]
                            nc.gpsimd.affine_select(out=tri, in_=tri, compare_op=ALU.is_ge, fill=0.0, base=0,
                                                    pattern=[[0, 2], [1, P]], channel_multiplier=-1).then_inc(masked, 1)
                passes(pool, body)

            @block.sync
            def _(sp):
                def load(stack, b, w, g, order, done):
                    for r, part in enumerate(order):
                        src = parts[w, g, b].rearrange("(j d) r t -> d j r t", d=HD)[:, :, part, :]
                        sp.dma_start(stack[r * HD:(r + 1) * HD].bitcast(F32), src).then_inc(done, 16)

                def load_q(g, b):
                    load(q_stack[:, b, :, :], b, 0, g, (0, 0, 1), q_loaded[b])

                def load_k(g, b):
                    load(k_stack[:, :, b * BLK:(b + 1) * BLK], b, 1, g, (0, 1, 0), k_loaded[b])

                def load_v(g, b):
                    sp.dma_start(v_grp[:, b * TB:(b + 1) * TB, :],
                                 v_all[:, b * TB:(b + 1) * TB, bass.ds(g * P, P)]).then_inc(v_loaded[b], 16)

                for b in range(NB):
                    load_q(0, b)
                    load_k(0, b)
                    load_v(0, b)
                with sp.Fori(0, G - 1) as g:
                    for b in range(NB - 1):
                        sp.wait_ge(values_done, g * NK + (VR + CUM_K[b + 1]))
                        load_q(g + 1, b)
                    for b in range(NB):
                        sp.wait_ge(values_done, g * NK + (VR + LAST_USE[b] + 1))
                        load_k(g + 1, b)
                        load_v(g + 1, b)
                    load_q(g + 1, NB - 1)

            @block.tensor
            def _(pe):
                pe.sem_inc(values_done, VR)
                pe.sem_inc(folded, C1)
                pe.wait_ge(consts_ready, 4)
                ring = []

                def wait_bank(g):
                    if len(ring) >= U3:
                        s, per, v = ring[-U3]
                        pe.wait_ge(s, g * per + v)

                def unit(g, gq, m, u, drained, r0=0):
                    j0, heads, qt, c = units(m)[u]
                    w = unit_width(m, units(m)[u])
                    if u == 0:
                        pe.wait_ge(q_loaded[m], gq * LOADS + LOADS)
                    if u == 0 or units(m)[u - 1][3] != c:
                        pe.wait_ge(k_loaded[c], gq * LOADS + LOADS)
                    wait_bank(g)
                    for n in range(heads):
                        to = ps_m[:, (r0 + len(ring)) % U3, n * w:(n + 1) * w]
                        last = nc.tensor.matmul(to, q_stack[0:MROW, m, j0 + n, qt * P:(qt + 1) * P],
                                                k_stack[0:MROW, j0 + n, c * BLK:c * BLK + w], start=True, stop=(c < m))
                        if c == m:
                            last = nc.tensor.matmul(to[:, w - P:w], ident16[:], above[:], start=False, stop=True)
                    last.then_inc(unit_ready, 1)
                    ring.append((unit_drained, NA, drained))

                def turn_maxima(g, m, n, r0=0):
                    wait_bank(g)
                    pe.wait_ge(max_ready, g * NB + n)
                    for qt in range(TB):
                        last = nc.tensor.transpose(ps_m[:, (r0 + len(ring)) % U3, qt * P:(qt + 1) * P],
                                                   turn_in[:, m % 2, qt, :], ident[:])
                    last.then_inc(max_turned, 1)
                    ring.append((max_placed, NB, n))

                for m in range(PH):
                    for u in range(AU[m]):
                        unit(0, 0, m, u, (m * AU[0]) + u + 1, R0)
                    turn_maxima(0, m, m + 1, R0)
                pe.wait_ge(ones_rows, 2)

                def body(g, last):
                    del ring[:]
                    ring.extend([(unit_drained, NA, U0)] * (U3 - 1) + [(max_placed, NB, PH)])
                    drained = U0
                    for step in orders[last]:
                        kind = step[0]
                        if kind == "scores":
                            _, t, j = step
                            b, i = TILES[t]
                            if t in CUM_K and j == 0:
                                pe.wait_ge(max_placed, g * NB + (b + 1))
                            n = HG * t + j
                            pe.wait_ge(exp_done, g * NE + (n + 1 if n >= S3 else S3))
                            lo = first_query(t)
                            nc.tensor.matmul(ps_s[:, n % S3, lo:BLK], k_stack[:, j, i * P:(i + 1) * P],
                                             q_stack[:, b, j, lo:BLK], start=True, stop=True).then_inc(scores_ready, 1)
                        elif kind == "fold":
                            upto = max(numbers[last][t] for t in numbers[last] if TILES[t][0] == step[1])
                            pe.wait_ge(added, g * NADD + upto)
                            for j in range(HG):
                                last_mm = nc.tensor.matmul(ps_l[j * HD:(j + 1) * HD, :], ones[:, :], acc[:, j, :],
                                                           start=False, stop=True)
                            last_mm.then_inc(folded, 1)
                        elif kind in ("sums", "values"):
                            t = step[1]
                            b, i = TILES[t]
                            first, final = t in CUM_K, t + 1 in CUM_K
                            if kind == "sums":
                                final = final and ("fold", b) not in orders[last]
                                if first:
                                    pe.wait_ge(sums_turned, g * NB + (C1 + b))
                                if DIAGONAL[t]:
                                    pe.wait_ge(masked, g * (2 * TB * NB) + masks_until(t))
                                else:
                                    pe.wait_ge(exp_done, g * NE + (S3 + HG * (t + 1)))
                            else:
                                if first:
                                    pe.wait_ge(y_copied, g * NB + (C1 + b))
                                if t == FIRST_USE[i // TB]:
                                    pe.wait_ge(v_loaded[i // TB], g * 16 + 16)
                            lo = first_query(t)
                            for j in range(HG):
                                rows = slice(j * HD, (j + 1) * HD)
                                to, lhs = (ps_l, ones[:, :]) if kind == "sums" else (ps_y, v_grp[:, i, rows])
                                last_mm = nc.tensor.matmul(to[rows, lo:BLK], lhs, probs[:, t % RING, j, lo:BLK],
                                                           start=first, stop=final)
                            if kind == "values":
                                last_mm.then_inc(values_done, 1)
                        elif kind == "max":
                            _, m, u = step
                            drained += 1
                            unit(g, g if m >= 2 else g + 1, m, u, drained)
                        elif kind == "turn":
                            turn_maxima(g, step[1], before(step[1]) + 1)
                passes(pe, body)

            @block.scalar
            def _(act):
                def place_maxima(g, m, n, r):
                    act.wait_ge(max_turned, g * NB + n)
                    nc.scalar.activation(q_stack[MROW:P, m, :, :],
                                         ps_m[MROW:P, r % U3, :].unsqueeze(1).to_broadcast([P - MROW, HG, BLK]),
                                         ACT.Copy).then_inc(max_placed, 1)

                act.sem_inc(y_copied, C1)
                act.sem_inc(exp_done, S3)
                act.wait_ge(const_step, 4)
                nc.scalar.activation(k_stack[MROW:P, 2:4, :], tail[MROW:P, 2:4].unsqueeze(2).to_broadcast([P - MROW, 2, T]),
                                     ACT.Copy).then_inc(ones_rows, 1)
                place_maxima(0, 0, 1, R0 + AU[0])
                place_maxima(0, 1, 2, R0 + AU[0] + 1 + AU[1])

                def body(g, last):
                    r = 0
                    for step in orders[last]:
                        if step[0] == "scores":
                            _, t, j = step
                            lo = first_query(t)
                            act.wait_ge(scores_ready, g * NE + (HG * t + j + 1))
                            if j == 0:
                                act.wait_ge(values_done, g * NK + (t + 1))
                                if t - RING in numbers[last]:
                                    act.wait_ge(added, g * NADD + numbers[last][t - RING])
                            nc.scalar.activation(probs[:, t % RING, j, lo:BLK], ps_s[:, (HG * t + j) % S3, lo:BLK], ACT.Exp,
                                                 scale=SCALE).then_inc(exp_done, 1)
                        elif step[0] == "copy":
                            b = step[1]
                            act.wait_ge(values_done, g * NK + (VR + CUM_K[b + 1]))
                            act.wait_ge(scaled, g * NB + (b + 1))
                            nc.scalar.activation(y_raw[:, b % 2, :], ps_y[:], ACT.Copy).then_inc(y_copied, 1)
                        elif step[0] == "max":
                            r += 1
                        elif step[0] == "turn":
                            place_maxima(g, step[1], before(step[1]) + 1, r)
                            r += 1
                passes(act, body)

            @block.vector
            def _(dve):
                dve.sem_inc(scaled, 2)
                dve.sem_inc(sums_turned, C1)
                dve.wait_ge(const_step, 4)
                nc.vector.tensor_copy(k_stack[MROW:P, 0:2, :],
                                      tail[MROW:P, 0:2].unsqueeze(2).to_broadcast([P - MROW, 2, T])).then_inc(ones_rows, 1)
                dve.wait_ge(consts_ready, 4)

                def drain_unit(g, m, u, r, drained):
                    j0, heads, qt, c = units(m)[u]
                    w = unit_width(m, units(m)[u])
                    dve.wait_ge(unit_ready, g * NA + drained)
                    nc.vector.tensor_reduce(part_max[:, m % 2, qt * HG + j0:qt * HG + j0 + heads, c],
                                            ps_m[:, r % U3, 0:heads * w].rearrange("p (n w) -> p n w", w=w), AX_X,
                                            ALU.max).then_inc(unit_drained, 1)

                def finish_maxima(g, m, n, drained):
                    buf = m % 2
                    dve.wait_ge(unit_drained, g * NA + drained)
                    nc.vector.tensor_reduce(neg_max[:, buf, :], part_max[:, buf, :, 0:m + 1], AX_X, ALU.max,
                                            negate=True).then_inc(max_step, 1)
                    dve.wait_ge(max_step, g * (2 * NB) + (2 * n - 1))
                    nc.vector.tensor_copy(neg_max_hi[:, buf, :], neg_max[:, buf, :]).then_inc(max_step, 1)
                    dve.wait_ge(max_step, g * (2 * NB) + 2 * n)
                    to = turn_in[:, buf, :, MROW:MROW + 2 * HG].rearrange("p t (j r) -> p t j r", r=2)
                    hi = neg_max_hi[:, buf, :].bitcast(F32).rearrange("p (t j) -> p t j", j=HG)
                    nc.vector.tensor_copy(to[:, :, :, 0], hi)
                    nc.vector.tensor_tensor(to[:, :, :, 1], neg_max[:, buf, :].rearrange("p (t j) -> p t j", j=HG), hi,
                                            ALU.subtract).then_inc(max_ready, 1)

                drained = 0
                for m in range(PH):
                    for u in range(AU[m]):
                        drained += 1
                        drain_unit(0, m, u, R0 + drained - 1 + m, drained)
                    finish_maxima(0, m, m + 1, drained)

                def body(g, last):
                    r, drained, folds = 0, U0, 0
                    for step in orders[last]:
                        kind = step[0]
                        folds += kind == "fold"
                        if kind == "add" and step[3] == "vector":
                            add(dve, nc.vector, g, last, step, folds)
                        if kind == "max":
                            drained += 1
                            drain_unit(g, step[1], step[2], r, drained)
                            r += 1
                        elif kind == "finish":
                            finish_maxima(g, step[1], before(step[1]) + 1, drained)
                        elif kind == "turn":
                            r += 1
                        elif kind == "copy":
                            dve.wait_ge(values_done, g * NK + (VR + CUM_K[step[1] + 1]))
                            nc.vector.transpose(sums_t[:], ps_l[:]).then_inc(sums_turned, 1)
                        elif kind == "invert":
                            b = step[1]
                            dve.wait_ge(sums_turned, g * NB + (C1 + b + 1))
                            nc.vector.reciprocal(inv_t[:], sums_t[:].rearrange("p (k c) -> p k c", c=HD)[:, :, 0]
                                                 ).then_inc(inverted, 1)
                            dve.wait_ge(inverted, g * (2 * NB) + (2 * b + 1))
                            nc.vector.transpose(inv_sum[:], inv_t[:].unsqueeze(2).to_broadcast([P, BLK // HD, HD])
                                                ).then_inc(inverted, 1)
                        elif kind == "scale":
                            b = step[1]
                            dve.wait_ge(y_copied, g * NB + (C1 + b + 1))
                            dve.wait_ge(inverted, g * (2 * NB) + 2 * (b + 1))
                            nc.vector.tensor_tensor(y_all[:, g, b * BLK:(b + 1) * BLK], y_raw[:, b % 2, :],
                                                    inv_sum[:], ALU.mult).then_inc(scaled, 1)
                passes(dve, body)


def output_program(nc, x, wo_hi, wo_lo, w_ffn, y_all, x1_all, w_ffn_sb):
    TT = T // P
    with ExitStack() as ctx:
        def sb(name, shape, dt):
            return ctx.enter_context(nc.sbuf_tensor("op_" + name, shape, dt))

        def sem(name):
            return ctx.enter_context(nc.semaphore("op_" + name))

        w_i8 = sb("w_i8", [P, 2, INTER // 4], I32)
        y_hi = sb("y_hi", [P, 4, KC, P], F32R)
        y_lo = sb("y_lo", [P, 4, KC, P], F32R)
        x_in = sb("x_in", [P, 2, C], F32)
        res = sb("res", [P, 2, C], F32)
        stats = sb("stats", [P, 2, 6], F32)
        mean_var = sb("mean_var", [P, 2, 2], F32)
        var_eps = sb("var_eps", [P, 2], F32)
        rstd = sb("rstd", [P, 2], F32)
        half = sb("half", [P, 1], F32)
        ps_o = ctx.enter_context(nc.psum_tensor("op_ps_o", [P, 4, C], F32))

        ffn_loaded, ffn_done = [sem("ffn_loaded0"), sem("ffn_loaded1")], sem("ffn_done")
        x_loaded = [sem("xin_loaded0"), sem("xin_loaded1")]
        half_set, passed = sem("half_set"), sem("passed")
        y_hi_done, y_lo_done, out_ready = sem("y_hi_done"), sem("y_lo_done"), sem("out_ready")
        res_done, stats_done, var_done, rstd_done, x1_done = (
            sem("res_done"), sem("stats_done"), sem("var_done"), sem("rstd_done"), sem("x1_done"))
        B2, B4 = 2, 4
        LEAD = 2

        def quads(eng, body):
            with eng.Fori(0, NCH // 4) as i:
                body(i * 4, False)
            body(NCH, True)

        with nc.Block() as block:
            @block.sync
            def _(sp):
                def body(n, last):
                    for j in range(4):
                        sp.wait_ge(res_done, n + (j + B4 - 1))
                        sp.dma_start(x_in[:, j % 2, :], x[n + j]).then_inc(x_loaded[j % 2], 16)
                        if not last:
                            sp.wait_ge(ffn_done, n + (j + 1))
                            sp.dma_start(w_i8[:, j % 2, :], w_ffn[n + j]).then_inc(ffn_loaded[j % 2], 16)
                quads(sp, body)

            @block.gpsimd
            def _(pool):
                nc.gpsimd.memset(half[:], -0.5).then_inc(half_set, 1)
                pool.wait_ge(half_set, 1)

                def low(n, j):
                    pool.wait_ge(y_hi_done, n + 1)
                    pool.sem_inc(passed, 1)
                    nc.gpsimd.tensor_tensor(y_lo[:, j, :, :], y_all[:, :, bass.ds(n * P, P)],
                                            y_hi[:, j, :, :].bitcast(F32), ALU.subtract).then_inc(y_lo_done, 1)

                def body(n, last):
                    for j in range(4):
                        if not (last and j + LEAD >= 4):
                            low(n + (j + LEAD), (j + LEAD) % 4)
                        r = j % 2
                        pool.wait_ge(var_done, n + (j + 1))
                        nc.gpsimd.tensor_tensor(rstd[:, r:r + 1], var_eps[:, r:r + 1], half[:], ALU.pow).then_inc(rstd_done, 1)

                for j in range(LEAD):
                    low(j, j)
                quads(pool, body)

            @block.tensor
            def _(pe):
                pe.sem_inc(out_ready, B4)
                with pe.Fori(0, TT // 4) as i:
                    for j in range(4):
                        pe.wait_ge(res_done, i * 4 + (j + 1))
                        pe.wait_ge(y_hi_done, i * 4 + (j + 1))
                        for n, (y, w) in enumerate(((y_hi, wo_hi), (y_hi, wo_lo), (y_lo, wo_hi))):
                            if n == 2:
                                pe.wait_ge(y_lo_done, i * 4 + (j + 1))
                            for k in range(KC):
                                last = nc.tensor.matmul(ps_o[:, j, :], y[:, j, k, :], w[:, :, k, :],
                                                        start=(n == 0 and k == 0), stop=(n == 2 and k == KC - 1))
                        last.then_inc(out_ready, 1)

            @block.scalar
            def _(act):
                act.sem_inc(ffn_done, B2)

                def high(n, j):
                    act.wait_ge(out_ready, n + 1)
                    nc.scalar.activation(y_hi[:, j, :, :], y_all[:, :, bass.ds(n * P, P)], ACT.Copy).then_inc(y_hi_done, 1)

                def body(n, last):
                    for j in range(4):
                        if not (last and j + LEAD >= 4):
                            high(n + (j + LEAD), (j + LEAD) % 4)
                        if not last:
                            act.wait_ge(ffn_loaded[j % 2], n * 8 + 16 * (j // 2 + 1))
                            nc.scalar.activation(w_ffn_sb[:, n + j, :], w_i8[:, j % 2, :].bitcast(I8),
                                                 ACT.Copy).then_inc(ffn_done, 1)

                for j in range(LEAD):
                    high(j, j)
                quads(act, body)

            @block.vector
            def _(dve):
                dve.sem_inc(res_done, B4)
                dve.sem_inc(x1_done, B2)

                def normalise(n, r):
                    dve.wait_ge(rstd_done, n + 1)
                    nc.vector.tensor_scalar(x1_all[:, n, :], res[:, r, :], mean_var[:, r, 0:1], rstd[:, r:r + 1],
                                            ALU.subtract, ALU.mult).then_inc(x1_done, 1)

                def body(n, last):
                    for j in range(4):
                        r = j % 2
                        dve.wait_ge(x_loaded[r], n * 8 + 16 * (j // 2 + 1))
                        dve.wait_ge(out_ready, n + (B4 + j + 1))
                        dve.wait_ge(x1_done, n + (j + 1))
                        nc.vector.tensor_tensor(res[:, r, :], ps_o[:, j, :], x_in[:, r, :], ALU.add).then_inc(res_done, 1)
                        dve.wait_ge(res_done, n + (B4 + j + 1))
                        nc.vector.bn_stats(stats[:, r, :], res[:, r, :]).then_inc(stats_done, 1)
                        dve.wait_ge(stats_done, n * 2 + (2 * j + 1))
                        dve.sem_inc(passed, 1)
                        nc.vector.bn_aggr(mean_var[:, r, :], stats[:, r, :]).then_inc(stats_done, 1)
                        dve.wait_ge(stats_done, n * 2 + (2 * j + 2))
                        nc.vector.tensor_scalar(var_eps[:, r:r + 1], mean_var[:, r, 1:2], LN_EPS, None,
                                                ALU.add).then_inc(var_done, 1)
                        if r == 1:
                            normalise(n + (j - 1), 0)
                            normalise(n + j, 1)

                quads(dve, body)


def ffn_program(nc, scales, s_down, out, x1_all, w_ffn_sb, ident, spare, x1t_hi, x1t_lo):
    with ExitStack() as ctx:
        def sb(name, shape, dt):
            return ctx.enter_context(nc.sbuf_tensor("ff_" + name, shape, dt))

        def sem(name):
            return ctx.enter_context(nc.semaphore("ff_" + name))

        s_gu = sb("s_gu", [P, 2, NO], F32)
        s_dn = sb("s_dn", [P, C], F32)
        x1t_hi = x1t_hi[:].rearrange("p k t c -> p k (t c)")
        x1t_lo = x1t_lo[:].rearrange("p k t c -> p k (t c)")
        gate = sb("gate", [P, 2, BLK], F32)
        fuse = sb("fuse", [P, 2, BLK], F32)
        fuse_hi = sb("fuse_hi", [P, 2, BLK], F32R)
        fuse_lo = sb("fuse_lo", [P, 2, BLK], F32R)
        z = spare[:, 0, :].rearrange("p (t c) -> p t c", c=C)
        result = spare[:, 1, :].rearrange("p (t c) -> p t c", c=C)
        x1_blk = spare[:, 2, :].rearrange("p (t c) -> p t c", c=C)
        stats = sb("stats2", [P, TB, 6], F32)
        mean_var = sb("mean_var2", [P, TB, 2], F32)
        var_eps = sb("var_eps2", [P, TB], F32)
        rstd = sb("rstd2", [P, TB], F32)
        half = sb("half2", [P, TB], F32)
        ps_gu = ctx.enter_context(nc.psum_tensor("ff_ps_gu", [P, 2, 2, BLK], F32))
        ps_d = ctx.enter_context(nc.psum_tensor("ff_ps_d", [P, TB, C], F32))

        consts_loaded, half_set, passed = sem("consts_loaded"), sem("half_set2"), sem("passed")
        blk_loaded, x1_turned, x1_hi_done, x1_lo_done = (
            sem("blk_loaded"), sem("x1_turned"), sem("x1_hi_done"), sem("x1_lo_done"))
        gate_ready, up_ready, gate_done, fuse_done, fuse_hi_done, fuse_lo_done, down_done = (
            sem("gate_ready"), sem("up_ready"), sem("gate_done"), sem("fuse_done"), sem("fuse_hi_done"),
            sem("fuse_lo_done"), sem("down_done"))
        z_scaled, z_done, stats_done, var_done, rstd_done, result_done, stored = (
            sem("z_scaled"), sem("z_done"), sem("stats_done2"), sem("var_done2"), sem("rstd_done2"),
            sem("result_done"), [sem(f"stored{t}") for t in range(TB)])
        B2 = 2

        w_gate = w_ffn_sb[:, 0:4, :]
        w_up = w_ffn_sb[:, 4:8, :]
        w_down = w_ffn_sb[:, 8:12, :].rearrange("p c (o n) -> p (c o) n", n=C)

        def blocks(eng, body):
            body(0, True)
            with eng.Fori(1, NB) as b:
                body(b, False)

        with nc.Block() as block:
            @block.sync
            def _(sp):
                for t in range(TB):
                    sp.sem_inc(stored[t], 16)
                sp.dma_start(s_gu[:], scales).then_inc(consts_loaded, 16)
                sp.dma_start(s_dn[:], s_down.unsqueeze(0).to_broadcast([P, C])).then_inc(consts_loaded, 16)

                def store(b):
                    for t in range(TB):
                        sp.wait_ge(result_done, b * TB + (t + 1))
                        sp.dma_start(out[b * TB + t], result[:, t, :]).then_inc(stored[t], 16)

                sp.dma_start(x1_blk, x1_all[:, TB:2 * TB, :]).then_inc(blk_loaded, 16)
                with sp.Fori(1, NB - 1) as b:
                    sp.wait_ge(x1_turned, b * KC + KC)
                    sp.dma_start(x1_blk, x1_all[:, bass.ds((b + 1) * TB, TB), :]).then_inc(blk_loaded, 16)
                    store(b - 1)
                store(NB - 2)
                store(NB - 1)
                for t in range(TB):
                    sp.wait_ge(stored[t], 16 * (NB + 1))

            @block.gpsimd
            def _(pool):
                pool.sem_inc(fuse_lo_done, B2)
                nc.gpsimd.memset(half[:], -0.5).then_inc(half_set, 1)
                pool.wait_ge(half_set, 1)

                def invert(n):
                    pool.wait_ge(var_done, n)
                    nc.gpsimd.tensor_tensor(rstd[:], var_eps[:], half[:], ALU.pow).then_inc(rstd_done, 1)

                def body(b, first):
                    for o in range(NO):
                        pool.wait_ge(fuse_hi_done, b * NO + (o + 1))
                        pool.wait_ge(down_done, b * NO + (o + 1))
                        nc.gpsimd.tensor_tensor(fuse_lo[:, o % 2, :], fuse[:, o % 2, :],
                                                fuse_hi[:, o % 2, :].bitcast(F32), ALU.subtract).then_inc(fuse_lo_done, 1)
                        if o == NORM_AT[2] and not first:
                            invert(b)
                blocks(pool, body)
                invert(NB)

            @block.tensor
            def _(pe):
                pe.sem_inc(down_done, B2)

                def down(o, base):
                    pe.wait_ge(fuse_hi_done, base + (o + 1))
                    for n, f in enumerate((fuse_hi, fuse_lo)):
                        if n == 1:
                            pe.wait_ge(fuse_lo_done, base + (B2 + o + 1))
                        for t in range(TB):
                            last = nc.tensor.matmul(ps_d[:, t, :], f[:, o % 2, t * P:(t + 1) * P], w_down[:, o, :],
                                                    start=(o == 0 and n == 0), stop=(o == NO - 1 and n == 1))
                    last.then_inc(down_done, 1)

                def body(b, first):
                    if not first:
                        pe.wait_ge(blk_loaded, b * 16)
                    tokens = x1_all[:, 0:TB, :] if first else x1_blk
                    for k in range(KC):
                        if not first:
                            pe.wait_ge((gate_done, fuse_done)[k // 2], b * NO + (k % 2 + 1))
                        for t in range(TB):
                            last = nc.tensor.transpose(ps_gu[:, k // 2, k % 2, t * P:(t + 1) * P],
                                                       tokens[:, t, k * P:(k + 1) * P], ident[:])
                        last.then_inc(x1_turned, 1)
                    if not first:
                        down(NO - 1, b * NO - NO)
                    for o in range(NO):
                        for s, (w, ready, free) in enumerate(((w_gate, gate_ready, gate_done), (w_up, up_ready, fuse_done))):
                            pe.wait_ge(free, b * NO + (o + 1))
                            if o < 2:
                                pe.wait_ge(x1_lo_done, b * KC + (2 * s + o + 1))
                            for n, m in enumerate((x1t_hi, x1t_lo)):
                                for k in range(KC):
                                    if o == 0 and s == 0:
                                        pe.wait_ge((x1_hi_done, x1_lo_done)[n], b * KC + (k + 1))
                                    last = nc.tensor.matmul(ps_gu[:, s, o % 2, :], w[:, k, o * P:(o + 1) * P], m[:, k, :],
                                                            start=(n == 0 and k == 0), stop=(n == 1 and k == KC - 1))
                            last.then_inc(ready, 1)
                        if o == 1:
                            pe.wait_ge(z_scaled, b * TB + TB)
                        if o >= 1:
                            down(o - 1, b * NO)
                blocks(pe, body)
                down(NO - 1, NB * NO - NO)

            @block.scalar
            def _(act):
                act.sem_inc(gate_done, B2)
                act.wait_ge(consts_loaded, 32)

                def body(b, first):
                    for k in range(KC):
                        act.wait_ge(x1_turned, b * KC + (k + 1))
                        nc.scalar.activation(x1t_hi[:, k, :], ps_gu[:, k // 2, k % 2, :], ACT.Copy).then_inc(x1_hi_done, 1)
                    for o in range(NO):
                        act.wait_ge(gate_ready, b * NO + (o + 1))
                        act.wait_ge(fuse_done, b * NO + (o + 1))
                        nc.scalar.activation(gate[:, o % 2, :], ps_gu[:, 0, o % 2, :], ACT.Silu,
                                             scale=s_gu[:, 0, o:o + 1]).then_inc(gate_done, 1)
                        act.wait_ge(fuse_done, b * NO + (B2 + o + 1))
                        act.wait_ge(down_done, b * NO + (o + 1))
                        nc.scalar.activation(fuse_hi[:, o % 2, :], fuse[:, o % 2, :], ACT.Copy).then_inc(fuse_hi_done, 1)
                blocks(act, body)

            @block.vector
            def _(dve):
                dve.sem_inc(z_scaled, TB)
                dve.sem_inc(fuse_done, B2)
                dve.wait_ge(consts_loaded, 32)

                def scale_down(n):
                    dve.wait_ge(down_done, n * NO + (B2 + NO))
                    if not isinstance(n, int) or n:
                        dve.wait_ge(result_done, n * TB)
                    for t in range(TB):
                        nc.vector.tensor_tensor(z[:, t, :], ps_d[:, t, :], s_dn[:], ALU.mult).then_inc(z_scaled, 1)

                def add_residual(n, t):
                    dve.wait_ge(z_scaled, n * TB + (TB + t + 1))
                    nc.vector.tensor_tensor(z[:, t, :], z[:, t, :], x1_all[:, n * TB + t, :], ALU.add).then_inc(z_done, 1)

                def statistics(n, t):
                    dve.wait_ge(z_done, n * TB + (t + 1))
                    nc.vector.bn_stats(stats[:, t, :], z[:, t, :]).then_inc(stats_done, 1)

                def aggregate(n):
                    dve.wait_ge(stats_done, n * (2 * TB) + TB)
                    dve.sem_inc(passed, 1)
                    for t in range(TB):
                        nc.vector.bn_aggr(mean_var[:, t, :], stats[:, t, :]).then_inc(stats_done, 1)
                    dve.wait_ge(stats_done, n * (2 * TB) + 2 * TB)
                    nc.vector.tensor_scalar(var_eps[:], mean_var[:, :, 1], LN_EPS, None, ALU.add).then_inc(var_done, 1)

                def normalise(n, t):
                    if t == 0:
                        dve.wait_ge(rstd_done, n + 1)
                    if not isinstance(n, int) or n:
                        dve.wait_ge(stored[t], n * 16 + 16)
                    nc.vector.tensor_scalar(result[:, t, :], z[:, t, :], mean_var[:, t, 0:1], rstd[:, t:t + 1],
                                            ALU.subtract, ALU.mult).then_inc(result_done, 1)

                def body(b, first):
                    for k in range(KC):
                        dve.wait_ge(x1_hi_done, b * KC + (k + 1))
                        nc.vector.tensor_tensor(x1t_lo[:, k, :], ps_gu[:, k // 2, k % 2, :], x1t_hi[:, k, :].bitcast(F32),
                                                ALU.subtract).then_inc(x1_lo_done, 1)
                    if not first:
                        scale_down(b - 1)
                    for o in range(NO):
                        dve.wait_ge(up_ready, b * NO + (o + 1))
                        dve.wait_ge(gate_done, b * NO + (B2 + o + 1))
                        dve.wait_ge(fuse_lo_done, b * NO + (o + 1))
                        nc.vector.scalar_tensor_tensor(fuse[:, o % 2, :], ps_gu[:, 1, o % 2, :], s_gu[:, 1, o:o + 1],
                                                       gate[:, o % 2, :], ALU.mult, ALU.mult).then_inc(fuse_done, 1)
                        if not first:
                            for at, step in zip(NORM_AT, (add_residual, statistics, None, normalise)):
                                if at <= o < at + TB and step:
                                    step(b - 1, o - at)
                            if o == NORM_AT[2]:
                                aggregate(b - 1)
                blocks(dve, body)
                scale_down(NB - 1)
                for t in range(TB):
                    add_residual(NB - 1, t)
                    statistics(NB - 1, t)
                aggregate(NB - 1)
                for t in range(TB):
                    normalise(NB - 1, t)


def build(nc, x, w_qkv, w_o, rope, w_ffn, scales, s_down, out):
    xt = x.rearrange("(t p) c -> t p c", p=P)
    with ExitStack() as ctx:
        def sb(name, shape, dt):
            return ctx.enter_context(nc.sbuf_tensor(name, shape, dt))

        ident = sb("ident", [P, P], F32)
        y_all = sb("y_all", [P, G, T], F32)
        parts = nc.dram_tensor("parts", (2, G, NB, P, 2, BLK), F32, kind="Internal").ap()
        wo_hi = sb("wo_hi", [P, G, KC, P], F32R)
        wo_lo = sb("wo_lo", [P, G, KC, P], F32R)
        with nc.sbuf_tensor("v_all", [P, T // P, C], F32) as v_all:
            project_program(nc, x.rearrange("(b t p) c -> b p t c", p=P, t=TB), w_qkv, w_o, rope, parts, v_all,
                            wo_hi, wo_lo, ident, y_all)
            attention_program(nc, parts, y_all, v_all, ident)
        x1_all = sb("x1_all", [P, T // P, C], F32)
        w_ffn_sb = sb("w_ffn_sb", [P, NCH, INTER], F32R)
        output_program(nc, xt, wo_hi, wo_lo, w_ffn, y_all, x1_all, w_ffn_sb)
        ffn_program(nc, scales, s_down, out.rearrange("(t p) c -> t p c", p=P), x1_all, w_ffn_sb, ident, y_all,
                    wo_hi, wo_lo)


def kernel(**inputs):
    import numpy as np
    import concourse.bacc as bacc
    from concourse.bass_utils import run_bass_kernel_spmd

    w = {n: np.asarray(inputs["L0_attn_w_" + n]) for n in "qkvo"}
    gate, up, down = (np.asarray(inputs["L0_ffn_w_" + n]) for n in ("gate", "up", "down"))
    inv_freq = np.float32(1) / np.power(np.float32(10000), np.arange(HD // 2, dtype=np.float32) / np.float32(HD // 2))
    angle = np.outer(inv_freq, np.arange(T, dtype=np.float32)).astype(np.float32)
    cos, sin = np.cos(angle), np.sin(angle)
    rope = np.stack([np.concatenate([cos, cos]), np.concatenate([-sin, sin])], axis=1)
    rope = np.tile(rope, (HG, 1, 1))
    arrays = {
        "x": np.asarray(inputs["L0_attn_x"]).reshape(T, C),
        "w_qkv": np.concatenate([w["q"], w["k"], w["v"]]).reshape(3 * G, P, C),
        "w_o": w["o"].reshape(G, P, C),
        "rope": rope.reshape(P, 2, NB, BLK).transpose(2, 0, 1, 3),
        "w_ffn": np.concatenate([gate.reshape(4, P, INTER), up.reshape(4, P, INTER),
                                 down.reshape(4, 4, P, C).transpose(0, 2, 1, 3).reshape(4, P, INTER)]),
        "scales": np.stack([np.asarray(inputs["L0_ffn_s_gate"]).reshape(NO, P),
                            np.asarray(inputs["L0_ffn_s_up"]).reshape(NO, P)]).transpose(2, 0, 1),
        "s_down": np.asarray(inputs["L0_ffn_s_down"]),
    }
    arrays = {n: np.ascontiguousarray(a) for n, a in arrays.items()}
    arrays["w_ffn"] = arrays["w_ffn"].view(np.int32)
    nc = bacc.Bacc("TRN2", target_bir_lowering=False, num_devices=1)
    args = {n: nc.dram_tensor(n, a.shape, mybir.dt.from_np(a.dtype), kind="ExternalInput").ap() for n, a in arrays.items()}
    out = nc.dram_tensor("out", (T, C), F32, kind="ExternalOutput").ap()
    build(nc, **args, out=out)
    r = run_bass_kernel_spmd(nc, [arrays], core_ids=[0])
    return r.results[0]["out"].reshape(1, T, C)
```
